# Optimizing a Trainium2 kernel written in Bass

```python
import numpy as np
import jax
import jax.numpy as jnp

def _softmax(x, axis=-1):
    return jax.nn.softmax(x, axis=axis)

def _gelu(x):
    return jax.nn.gelu(x, approximate=True)

def _silu(x):
    return jax.nn.silu(x)

def _sigmoid(x):
    return jax.nn.sigmoid(x)

def _layernorm(x, axis=-1, eps=1e-05):
    m = jnp.mean(x, axis=axis, keepdims=True)
    v = jnp.var(x, axis=axis, keepdims=True)
    return (x - m) / jnp.sqrt(v + eps)

def _scatter_add(tgt, idx, src, axis=0):
    return tgt.at[idx].add(src)

def _segment_sum(src, seg, n):
    return jax.ops.segment_sum(src, seg, n)
kernel_name = 'mk_dlrm_tower_d1_rec_r8_e531a7'

def setup_inputs(seed: int=0):
    np.random.seed(seed)
    _w = jnp.asarray

    def _rec_inputs():
        import jax
        import jax.numpy as jnp
        _tk = jax.random.key(seed)
        dense_ctx = jax.random.normal(jax.random.fold_in(_tk, 190), (512, 16), jnp.float32)
        ids = jnp.stack([jax.random.randint(jax.random.fold_in(_tk, 200 + f), (512,), 0, v, jnp.int32) for f, v in enumerate([1250, 12500, 1250, 1000, 125000, 1000, 12500, 12500, 1000, 1250, 12500, 1250, 1000, 1250, 1000, 1000, 12500, 1250, 12500, 1250, 125000, 1000, 1000, 12500, 1000, 1250, 1250, 1250, 12500, 12500, 12500, 125000, 12500, 12500, 12500, 125000, 1000, 125000, 12500])], axis=1)
        tbl_0 = 0.05 * jax.random.normal(jax.random.fold_in(_tk, 500 + 0), (1250, 16), jnp.float32)
        tbl_1 = 0.05 * jax.random.normal(jax.random.fold_in(_tk, 500 + 1), (12500, 16), jnp.float32)
        tbl_2 = 0.05 * jax.random.normal(jax.random.fold_in(_tk, 500 + 2), (1250, 16), jnp.float32)
        tbl_3 = 0.05 * jax.random.normal(jax.random.fold_in(_tk, 500 + 3), (1000, 16), jnp.float32)
        tbl_4 = 0.05 * jax.random.normal(jax.random.fold_in(_tk, 500 + 4), (125000, 16), jnp.float32)
        tbl_5 = 0.05 * jax.random.normal(jax.random.fold_in(_tk, 500 + 5), (1000, 16), jnp.float32)
        tbl_6 = 0.05 * jax.random.normal(jax.random.fold_in(_tk, 500 + 6), (12500, 16), jnp.float32)
        tbl_7 = 0.05 * jax.random.normal(jax.random.fold_in(_tk, 500 + 7), (12500, 16), jnp.float32)
        tbl_8 = 0.05 * jax.random.normal(jax.random.fold_in(_tk, 500 + 8), (1000, 16), jnp.float32)
        tbl_9 = 0.05 * jax.random.normal(jax.random.fold_in(_tk, 500 + 9), (1250, 16), jnp.float32)
        tbl_10 = 0.05 * jax.random.normal(jax.random.fold_in(_tk, 500 + 10), (12500, 16), jnp.float32)
        tbl_11 = 0.05 * jax.random.normal(jax.random.fold_in(_tk, 500 + 11), (1250, 16), jnp.float32)
        tbl_12 = 0.05 * jax.random.normal(jax.random.fold_in(_tk, 500 + 12), (1000, 16), jnp.float32)
        tbl_13 = 0.05 * jax.random.normal(jax.random.fold_in(_tk, 500 + 13), (1250, 16), jnp.float32)
        tbl_14 = 0.05 * jax.random.normal(jax.random.fold_in(_tk, 500 + 14), (1000, 16), jnp.float32)
        tbl_15 = 0.05 * jax.random.normal(jax.random.fold_in(_tk, 500 + 15), (1000, 16), jnp.float32)
        tbl_16 = 0.05 * jax.random.normal(jax.random.fold_in(_tk, 500 + 16), (12500, 16), jnp.float32)
        tbl_17 = 0.05 * jax.random.normal(jax.random.fold_in(_tk, 500 + 17), (1250, 16), jnp.float32)
        tbl_18 = 0.05 * jax.random.normal(jax.random.fold_in(_tk, 500 + 18), (12500, 16), jnp.float32)
        tbl_19 = 0.05 * jax.random.normal(jax.random.fold_in(_tk, 500 + 19), (1250, 16), jnp.float32)
        tbl_20 = 0.05 * jax.random.normal(jax.random.fold_in(_tk, 500 + 20), (125000, 16), jnp.float32)
        tbl_21 = 0.05 * jax.random.normal(jax.random.fold_in(_tk, 500 + 21), (1000, 16), jnp.float32)
        tbl_22 = 0.05 * jax.random.normal(jax.random.fold_in(_tk, 500 + 22), (1000, 16), jnp.float32)
        tbl_23 = 0.05 * jax.random.normal(jax.random.fold_in(_tk, 500 + 23), (12500, 16), jnp.float32)
        tbl_24 = 0.05 * jax.random.normal(jax.random.fold_in(_tk, 500 + 24), (1000, 16), jnp.float32)
        tbl_25 = 0.05 * jax.random.normal(jax.random.fold_in(_tk, 500 + 25), (1250, 16), jnp.float32)
        tbl_26 = 0.05 * jax.random.normal(jax.random.fold_in(_tk, 500 + 26), (1250, 16), jnp.float32)
        tbl_27 = 0.05 * jax.random.normal(jax.random.fold_in(_tk, 500 + 27), (1250, 16), jnp.float32)
        tbl_28 = 0.05 * jax.random.normal(jax.random.fold_in(_tk, 500 + 28), (12500, 16), jnp.float32)
        tbl_29 = 0.05 * jax.random.normal(jax.random.fold_in(_tk, 500 + 29), (12500, 16), jnp.float32)
        tbl_30 = 0.05 * jax.random.normal(jax.random.fold_in(_tk, 500 + 30), (12500, 16), jnp.float32)
        tbl_31 = 0.05 * jax.random.normal(jax.random.fold_in(_tk, 500 + 31), (125000, 16), jnp.float32)
        tbl_32 = 0.05 * jax.random.normal(jax.random.fold_in(_tk, 500 + 32), (12500, 16), jnp.float32)
        tbl_33 = 0.05 * jax.random.normal(jax.random.fold_in(_tk, 500 + 33), (12500, 16), jnp.float32)
        tbl_34 = 0.05 * jax.random.normal(jax.random.fold_in(_tk, 500 + 34), (12500, 16), jnp.float32)
        tbl_35 = 0.05 * jax.random.normal(jax.random.fold_in(_tk, 500 + 35), (125000, 16), jnp.float32)
        tbl_36 = 0.05 * jax.random.normal(jax.random.fold_in(_tk, 500 + 36), (1000, 16), jnp.float32)
        tbl_37 = 0.05 * jax.random.normal(jax.random.fold_in(_tk, 500 + 37), (125000, 16), jnp.float32)
        tbl_38 = 0.05 * jax.random.normal(jax.random.fold_in(_tk, 500 + 38), (12500, 16), jnp.float32)
        _rk = jax.random.fold_in(_tk, 7)
        W_top1 = 0.05 * jax.random.normal(jax.random.fold_in(_tk, 801), (400, 512), jnp.float32)
        W_top2 = 0.0441942 * jax.random.normal(jax.random.fold_in(_tk, 802), (512, 256), jnp.float32)
        W_top3 = 0.0625 * jax.random.normal(jax.random.fold_in(_tk, 803), (256, 1), jnp.float32)
        b_top1 = jnp.zeros((512,), jnp.float32)
        b_top2 = jnp.zeros((256,), jnp.float32)
        return (dense_ctx, ids, tbl_0, tbl_1, tbl_2, tbl_3, tbl_4, tbl_5, tbl_6, tbl_7, tbl_8, tbl_9, tbl_10, tbl_11, tbl_12, tbl_13, tbl_14, tbl_15, tbl_16, tbl_17, tbl_18, tbl_19, tbl_20, tbl_21, tbl_22, tbl_23, tbl_24, tbl_25, tbl_26, tbl_27, tbl_28, tbl_29, tbl_30, tbl_31, tbl_32, tbl_33, tbl_34, tbl_35, tbl_36, tbl_37, tbl_38, W_top1, b_top1, W_top2, b_top2, W_top3)
    dense_ctx, ids, tbl_0, tbl_1, tbl_2, tbl_3, tbl_4, tbl_5, tbl_6, tbl_7, tbl_8, tbl_9, tbl_10, tbl_11, tbl_12, tbl_13, tbl_14, tbl_15, tbl_16, tbl_17, tbl_18, tbl_19, tbl_20, tbl_21, tbl_22, tbl_23, tbl_24, tbl_25, tbl_26, tbl_27, tbl_28, tbl_29, tbl_30, tbl_31, tbl_32, tbl_33, tbl_34, tbl_35, tbl_36, tbl_37, tbl_38, W_top1, b_top1, W_top2, b_top2, W_top3 = _rec_inputs()

    def _L0_rec_setup():
        import jax, jax.numpy as jnp
        import numpy as np
        B, F0, D = (256, 39, 16)
        CROSS = [128, 128, 128]
        key = jax.random.key(seed)
        k0, k1, k2, k3 = jax.random.split(key, 4)
        inputs = jax.random.normal(k0, (B, F0, D), dtype=jnp.float32)
        f0 = jax.random.normal(k1, (F0 * F0, CROSS[0]), dtype=jnp.float32) * 0.05
        f1 = jax.random.normal(k2, (CROSS[0] * F0, CROSS[1]), dtype=jnp.float32) * 0.05
        f2 = jax.random.normal(k3, (CROSS[1] * F0, CROSS[2]), dtype=jnp.float32) * 0.05
        return {'inputs': inputs, 'f0': f0, 'f1': f1, 'f2': f2}
    _L0_rec_all = _L0_rec_setup()
    _L0_rec_in = {k: v for k, v in _L0_rec_all.items() if k in ('f0', 'f1', 'f2')}
    del _L0_rec_all
    return {'dense_ctx': dense_ctx, 'ids': ids, 'tbl_0': tbl_0, 'tbl_1': tbl_1, 'tbl_2': tbl_2, 'tbl_3': tbl_3, 'tbl_4': tbl_4, 'tbl_5': tbl_5, 'tbl_6': tbl_6, 'tbl_7': tbl_7, 'tbl_8': tbl_8, 'tbl_9': tbl_9, 'tbl_10': tbl_10, 'tbl_11': tbl_11, 'tbl_12': tbl_12, 'tbl_13': tbl_13, 'tbl_14': tbl_14, 'tbl_15': tbl_15, 'tbl_16': tbl_16, 'tbl_17': tbl_17, 'tbl_18': tbl_18, 'tbl_19': tbl_19, 'tbl_20': tbl_20, 'tbl_21': tbl_21, 'tbl_22': tbl_22, 'tbl_23': tbl_23, 'tbl_24': tbl_24, 'tbl_25': tbl_25, 'tbl_26': tbl_26, 'tbl_27': tbl_27, 'tbl_28': tbl_28, 'tbl_29': tbl_29, 'tbl_30': tbl_30, 'tbl_31': tbl_31, 'tbl_32': tbl_32, 'tbl_33': tbl_33, 'tbl_34': tbl_34, 'tbl_35': tbl_35, 'tbl_36': tbl_36, 'tbl_37': tbl_37, 'tbl_38': tbl_38, 'W_top1': W_top1, 'b_top1': b_top1, 'W_top2': W_top2, 'b_top2': b_top2, 'W_top3': W_top3, 'L0_rec_f0': _L0_rec_in['f0'], 'L0_rec_f1': _L0_rec_in['f1'], 'L0_rec_f2': _L0_rec_in['f2']}

def reference(dense_ctx, ids, tbl_0, tbl_1, tbl_2, tbl_3, tbl_4, tbl_5, tbl_6, tbl_7, tbl_8, tbl_9, tbl_10, tbl_11, tbl_12, tbl_13, tbl_14, tbl_15, tbl_16, tbl_17, tbl_18, tbl_19, tbl_20, tbl_21, tbl_22, tbl_23, tbl_24, tbl_25, tbl_26, tbl_27, tbl_28, tbl_29, tbl_30, tbl_31, tbl_32, tbl_33, tbl_34, tbl_35, tbl_36, tbl_37, tbl_38, W_top1, b_top1, W_top2, b_top2, W_top3, L0_rec_f0, L0_rec_f1, L0_rec_f2):
    import jax
    import jax.numpy as jnp

    def _L0_rec_ref(inputs, f0, f1, f2):
        import jax, jax.numpy as jnp
        import numpy as np
        B, F0, D = (256, 39, 16)
        CROSS = [128, 128, 128]
        filters = [f0, f1, f2]
        x0 = inputs
        xk = inputs
        outs = []
        for W in filters:
            b, f, d = x0.shape
            g = xk.shape[1]
            z = jnp.einsum('bfd,bgd->bfgd', x0, xk).reshape(b, f * g, d)
            cur = jnp.einsum('bpd,pm->bmd', z, W)
            outs.append(cur)
            xk = cur
        result = jnp.concatenate(outs, axis=1)
        return jnp.sum(result, axis=-1)
    e = jnp.stack([tbl_0[ids[:, 0]], tbl_1[ids[:, 1]], tbl_2[ids[:, 2]], tbl_3[ids[:, 3]], tbl_4[ids[:, 4]], tbl_5[ids[:, 5]], tbl_6[ids[:, 6]], tbl_7[ids[:, 7]], tbl_8[ids[:, 8]], tbl_9[ids[:, 9]], tbl_10[ids[:, 10]], tbl_11[ids[:, 11]], tbl_12[ids[:, 12]], tbl_13[ids[:, 13]], tbl_14[ids[:, 14]], tbl_15[ids[:, 15]], tbl_16[ids[:, 16]], tbl_17[ids[:, 17]], tbl_18[ids[:, 18]], tbl_19[ids[:, 19]], tbl_20[ids[:, 20]], tbl_21[ids[:, 21]], tbl_22[ids[:, 22]], tbl_23[ids[:, 23]], tbl_24[ids[:, 24]], tbl_25[ids[:, 25]], tbl_26[ids[:, 26]], tbl_27[ids[:, 27]], tbl_28[ids[:, 28]], tbl_29[ids[:, 29]], tbl_30[ids[:, 30]], tbl_31[ids[:, 31]], tbl_32[ids[:, 32]], tbl_33[ids[:, 33]], tbl_34[ids[:, 34]], tbl_35[ids[:, 35]], tbl_36[ids[:, 36]], tbl_37[ids[:, 37]], tbl_38[ids[:, 38]]], axis=1)
    z = _L0_rec_ref(e, L0_rec_f0, L0_rec_f1, L0_rec_f2)
    z = z.reshape(z.shape[0], -1)
    h = jnp.concatenate([z, dense_ctx], axis=1)
    h = jnp.maximum(h @ W_top1 + b_top1, 0.0)
    h = jnp.maximum(h @ W_top2 + b_top2, 0.0)
    y = h @ W_top3
    return y

_drawn_inputs = setup_inputs


def setup_inputs(seed=0):
    import zlib

    import numpy as np

    out = dict(_drawn_inputs(seed))
    spreads = {'b_top1': (0.0, 0.571), 'b_top2': (0.0, 0.1)}
    factors = {'tbl_0': 4.704,
     'tbl_1': 4.91,
     'tbl_2': 4.551,
     'tbl_3': 4.716,
     'tbl_4': 4.879,
     'tbl_5': 4.936,
     'tbl_6': 4.791,
     'tbl_7': 4.743,
     'tbl_8': 4.876,
     'tbl_9': 4.394,
     'tbl_10': 4.827,
     'tbl_11': 4.77,
     'tbl_12': 4.53,
     'tbl_13': 4.608,
     'tbl_14': 4.877,
     'tbl_15': 4.873,
     'tbl_16': 5.605,
     'tbl_17': 4.876,
     'tbl_18': 5.076,
     'tbl_19': 5.292,
     'tbl_20': 4.762,
     'tbl_21': 4.645,
     'tbl_22': 4.565,
     'tbl_23': 4.86,
     'tbl_24': 4.855,
     'tbl_25': 4.538,
     'tbl_26': 4.905,
     'tbl_27': 5.127,
     'tbl_28': 4.712,
     'tbl_29': 5.127,
     'tbl_30': 5.057,
     'tbl_31': 4.163,
     'tbl_32': 4.899,
     'tbl_33': 5.108,
     'tbl_34': 4.672,
     'tbl_35': 4.995,
     'tbl_36': 4.852,
     'tbl_37': 5.084,
     'tbl_38': 5.108,
     'L0_rec_f1': 4.948,
     'L0_rec_f2': 8.0}
    for name, (base, spread) in spreads.items():
        noise = np.random.default_rng([zlib.crc32(name.encode()), seed]).standard_normal(out[name].shape)
        drawn = base * np.exp(spread * noise) if base else spread * noise
        out[name] = jnp.asarray(drawn.astype(out[name].dtype))
    for name, factor in factors.items():
        out[name] = (out[name] * factor).astype(out[name].dtype)
    return out
```

```python
from contextlib import ExitStack

import numpy as np

import concourse.bass as bass
from concourse import mybir

F32 = mybir.dt.float32
F32R = mybir.dt.float32r
I32 = mybir.dt.int32
ALU = mybir.AluOpType
ACT = mybir.ActivationFunctionType
AX_X = mybir.AxisListType.X

B = 512
F = 39
D = 16
M = 128
P = 128
FEATURES = 3 * M + 16
H1, H2 = 512, 256

COLS = 512
BLK = 8
GROUPS = B // P
TPG = 4
TILES = GROUPS * TPG
NBLK = COLS // P
LO = 64
KX = LO + F
FG = 10
ROT = 4
C0 = 7
FS = F + 1

SEL_REP = 0
SEL_A = FG
SEL_B = FG + 1
NSEL = FG + 1 + C0
SEL_COLS = NSEL * P + FS

UNITS = 2 * FG + 4
ITEMS = FG + 1 + C0
AHEAD = 4


def items_of(step):
    cross = [("L1", g) for g in range(FG)]
    if step.place == TILES - 1:
        return cross
    if step.place < 0:
        return [None] * FG + [("A", 0)] + [("B", c) for c in range(C0)]
    first = 8 if step.q == TPG - 1 else 4
    return cross[:first] + [("A", 0)] + [("B", c) for c in range(C0)] + cross[first:]


def units_of(item):
    if item is None:
        return [None, None]
    kind, n = item
    if kind == "L1":
        return [("L1", n, 0), ("L1", n, 1)]
    if kind == "B" and (n % 2 == 1 or n == C0 - 1):
        return [("L0", n // 2, 0)]
    return []


def unit_list(step):
    return [u for it in items_of(step) for u in units_of(it)]


def unit_at(step, k):
    return sum(len(units_of(it)) for it in items_of(step)[:k])


def on_pool(unit):
    kind, n, half = unit
    if kind == "L0":
        return n in (0, 2)
    return half == 0


class Step:

    def __init__(self, value, place, group):
        self.value, self.place, self.group = value, place, group

    @property
    def q(self):
        return self.place % TPG

    def back(self, n=1):
        return Step(self.value - n, self.place - n, None)


def units_through(step, u):
    return step.value * UNITS + (4 + u + 1)


def lows_through(step, u):
    while u < 0:
        step, u = step.back(), u + UNITS
    units = unit_list(step)
    pool = on_pool(units[u])
    layer0 = [("L0", n, 0) for n in range(4)]
    first = sum(on_pool(x) == pool for x in layer0)
    every = first + sum(on_pool(("L1", g, h)) == pool for g in range(FG) for h in range(2))
    here = sum(x is not None and on_pool(x) == pool for x in units[:u + 1])
    if step.place < 0:
        return pool, here
    return pool, step.value * every + (first + here)


def reps_through(step, k):
    return step.value * ITEMS + (1 + C0 + k + 1)


def products_through(step, k):
    names = items_of(step)[:k + 1]
    here = sum(it is not None and it[0] != "A" for it in names)
    if step.place < 0:
        return here
    return step.value * (ITEMS - 1) + (C0 + here)


def slot(u):
    return u % 4


def bank(k):
    return (1 + C0 + k) % 3


S_AT = {0: (1, 2, 3, 4, 5), 1: (1, 2, 3, 4, 5), 2: (1, 2, 3, 4, 5), 3: (3, 4, 5, 6, 7)}
L2_AT = (6, 8, 10)
TOP_AT = (12, 14, 16)
PREP_AT = (0, 0, 1, 2)
X0D_AT = (10, 11)
L2_CUT = (0, 13, 26, F)
LAG = 2
GATHERS = F // 3


def cross_network(nc, ids, tables, w0a, w0b, w1, w2, wt1, bt1, wt2, bt2, wt3, dense_t, selectors, identity, mask8, out):
    with ExitStack() as ctx:
        def sb(name, shape, dt=F32):
            return ctx.enter_context(nc.sbuf_tensor(name, shape, dt))

        def ps(name, shape):
            return ctx.enter_context(nc.psum_tensor(name, shape, F32))

        def sem(name):
            return ctx.enter_context(nc.semaphore(name))

        w1_hi = sb("w1_hi", [P, FG * ROT, M], F32R)
        w1_lo = sb("w1_lo", [P, FG * ROT, M], F32R)
        w0_hi = sb("w0_hi", [P, C0, M], F32R)
        w0_lo = sb("w0_lo", [P, C0, M], F32R)
        w2_sb = sb("w2_sb", [P, F, M])
        wt1_sb = sb("wt1_sb", [P, 4, H1])
        wt2_sb = sb("wt2_sb", [P, H1 // P, H2])
        wt3_sb = sb("wt3_sb", [P, H2 // P])
        bt1_sb = sb("bt1_sb", [P, H1 // P])
        bt2_sb = sb("bt2_sb", [P, H2 // P])
        sel = sb("sel", [KX, SEL_COLS], F32R)
        ident = sb("ident", [P, P])
        mask_sb = sb("mask_sb", [P, BLK])
        ids_now = sb("ids_now", [P, F], I32)
        emb = sb("emb", [P, F, D])
        x0_cols = sb("x0_cols", [KX, TPG * COLS], F32R)
        x0_last = sb("x0_last", [KX, COLS], F32R)
        x0_three = sb("x0_three", [P, COLS])
        x0_rows = sb("x0_rows", [P, TPG * NBLK, FS])
        z = sb("z", [P, 4, 2, COLS])
        z_hi = sb("z_hi", [P, 4, 2, COLS], F32R)
        z_lo = sb("z_lo", [P, 4, 2, COLS], F32R)
        x1_rot = sb("x1_rot", [P, 2, ROT, COLS])
        x2_sb = sb("x2_sb", [P, COLS])
        x2_rows = sb("x2_rows", [P, NBLK, P])
        diag = sb("diag", [P, NBLK, BLK, FS])
        s_sb = sb("s_sb", [P, FS, P])
        r0_tile = sb("r0_tile", [P, 2, NBLK * BLK])
        r0_sb = sb("r0_sb", [P, P])
        r2_sb = sb("r2_sb", [P, P])
        dense_sb = sb("dense_sb", [16, P])
        h1_sb = x2_rows
        h2_sb = sb("h2_sb", [P, H2 // P, P])
        y_sb = sb("y_sb", [1, P])

        w1_raw = s_sb
        zf = z[:, :, :, :].rearrange("p a b n -> p (a b n)")
        w0a_raw = x1_rot[:, 0, :, :].rearrange("p a n -> p (a n)")[:, 0:C0 * M].rearrange("p (c m) -> p c m", c=C0)
        w0b_raw = x1_rot[:, 0, :, :].rearrange("p a n -> p (a n)")[:, C0 * M:2 * C0 * M].rearrange("p (c m) -> p c m", c=C0)
        w0_raw = x1_rot[:, 1, :, :].rearrange("p a n -> p (a n)")[:, 0:C0 * M].rearrange("p (c m) -> p c m", c=C0)
        sel_raw = zf[0:KX, 0:SEL_COLS]

        rep = [ps(f"rep{i}", [P, COLS]) for i in range(3)]
        acc0 = ps("acc0", [P, COLS])
        acc1 = [ps(f"acc1_{i}", [P, COLS]) for i in range(2)]
        side = [ps("side_t", [P, COLS]), ps("side_s", [P, COLS])]

        ids_in = sem("ids_in")
        weights_in = sem("weights_in")
        w1_in = sem("w1_in")
        top_in = sem("top_in")
        dense_in = sem("dense_in")
        blank = sem("blank")
        w0_sum = sem("w0_sum")
        w_hi_done = sem("w_hi_done")
        w_lo_done = sem("w_lo_done")
        gathered = sem("gathered")
        prep_t = sem("prep_t")
        cols_hi = sem("cols_hi")
        cols_lo = sem("cols_lo")
        rows_t = sem("rows_t")
        rows_in = sem("rows_in")
        last_in = sem("last_in")
        rep_ready = sem("rep_ready")
        three_in = sem("three_in")
        prod = sem("prod")
        hi_done = sem("hi_done")
        lo_pool = sem("lo_pool")
        lo_dve = sem("lo_dve")
        unit_done = sem("unit_done")
        x1_in = sem("x1_in")
        x1_turned = sem("x1_turned")
        r0_done = sem("r0_done")
        r0_in = sem("r0_in")
        x2_in = sem("x2_in")
        x2_t = sem("x2_t")
        x2_rows_in = sem("x2_rows_in")
        diag_in = sem("diag_in")
        s_ready = sem("s_ready")
        s_in = sem("s_in")
        r2_ready = sem("r2_ready")
        r2_in = sem("r2_in")
        h1_ready = sem("h1_ready")
        h1_in = sem("h1_in")
        h2_ready = sem("h2_ready")
        h2_in = sem("h2_in")
        y_ready = sem("y_ready")
        y_in = sem("y_in")
        y_out = sem("y_out")

        lo_sem = {True: lo_pool, False: lo_dve}
        block = ctx.enter_context(nc.Block())

        def run_steps(eng, step_of):
            for n in range(TPG):
                step_of(Step(n, n, 0))
            with eng.Fori(1, GROUPS - 1) as g:
                for n in range(TPG):
                    step_of(Step(g * TPG + n, TPG + n, g))
            for n in range(TILES - TPG, TILES):
                step_of(Step(n, n, GROUPS - 1))

        def wait_low(eng, step, u):
            pool, n = lows_through(step, u)
            eng.wait_ge(lo_sem[pool], n)

        @block.sync
        def _(sp):
            def turn_x1(value, b):
                sp.wait_ge(x1_in, value + 1)
                for r in range(1, ROT):
                    cut = P - 32 * r
                    sp.dma_start(x1_rot[0:cut, b, r, :], x1_rot[32 * r:P, b, 0, :]).then_inc(x1_turned, 16)
                    sp.dma_start(x1_rot[cut:P, b, r, :], x1_rot[0:32 * r, b, 0, :]).then_inc(x1_turned, 16)

            def store_y(g):
                sp.wait_ge(y_in, g + 1)
                sp.dma_start(out[bass.ds(g * P, P), :].rearrange("b o -> o b"), y_sb[:, :]).then_inc(y_out, 16)

            def load_dense(g):
                sp.dma_start(dense_sb[:, :], dense_t[:, bass.ds(g * P, P)]).then_inc(dense_in, 16)

            def load_ids(g):
                sp.dma_start(ids_now[:, :], ids[bass.ds(g * P, P), :]).then_inc(ids_in, 16)

            load_ids(0)
            sp.dma_start(sel_raw, selectors[0:KX, :]).then_inc(weights_in, 16)
            sp.dma_start(w0a_raw, w0a).then_inc(weights_in, 16)
            sp.dma_start(w0b_raw, w0b).then_inc(weights_in, 16)
            sp.dma_start(ident[:, :], identity).then_inc(weights_in, 16)
            sp.dma_start(mask_sb[:, :], mask8).then_inc(weights_in, 16)
            sp.dma_start(w1_raw[:, :, :], w1).then_inc(w1_in, 16)
            sp.dma_start(w2_sb[:, :, :], w2).then_inc(top_in, 16)
            sp.dma_start(wt1_sb[:, 0:3, :], wt1[0:3 * P, :].rearrange("(c p) n -> p c n", p=P)).then_inc(top_in, 16)
            sp.dma_start(wt1_sb[0:16, 3, :], wt1[3 * P:FEATURES, :]).then_inc(top_in, 16)
            sp.dma_start(wt2_sb[:, :, :], wt2.rearrange("(c p) n -> p c n", p=P)).then_inc(top_in, 16)
            sp.dma_start(wt3_sb[:, :], wt3).then_inc(top_in, 16)
            sp.dma_start(bt1_sb[:, :], bt1).then_inc(top_in, 16)
            sp.dma_start(bt2_sb[:, :], bt2).then_inc(top_in, 16)
            load_dense(0)
            turn_x1(0, 0)

            def one_step(step):
                if step.q == 0 and step.place < TILES - TPG:
                    sp.wait_ge(gathered, step.group * (16 * F) + 16 * F)
                    load_ids(step.group + 1)
                if step.place < TILES - 1:
                    turn_x1(step.value + 1, (step.place + 1) % 2)
                if step.q == 0 and step.place > 0:
                    store_y(step.group - 1)
                    sp.wait_ge(y_out, step.group * 16)
                    load_dense(step.group)

            run_steps(sp, one_step)
            store_y(GROUPS - 1)
            sp.wait_ge(y_out, 16 * GROUPS)

        @block.gpsimd
        def _(pool):
            def gather(f):
                pool.indirect_dma_start(
                    out=emb[:, f, :], out_offset=None, in_=tables[f][:, :],
                    in_offset=bass.IndirectOffsetOnAxis(ap=ids_now[:, f:f + 1], axis=0),
                ).then_inc(gathered, 16)

            def low_part(step, u, unit):
                pool.wait_ge(hi_done, units_through(step, u))
                if step.place >= 0:
                    pool.wait_ge(unit_done, units_through(step, u - 4))
                s = slot(u)
                n = 1 if unit[:2] == ("L0", 3) else 2
                pool.tensor_tensor(z_lo[:, s, 0:n, :], z[:, s, 0:n, :], z_hi[:, s, 0:n, :].bitcast(F32),
                                   ALU.subtract).then_inc(lo_pool, 1)

            def one_step(step):
                todo = []
                if step.q < 3 and step.place < TILES - TPG:
                    if step.q == 0:
                        pool.wait_ge(prep_t, step.group * 4 + 4)
                        pool.wait_ge(ids_in, step.group * 16 + 32)
                    todo = list(range(step.q * GATHERS, (step.q + 1) * GATHERS))
                for u, unit in enumerate(unit_list(step)):
                    if on_pool(unit):
                        low_part(step, u, unit)
                        if todo:
                            gather(todo.pop(0))
                for f in todo:
                    gather(f)

            pool.wait_ge(ids_in, 16)
            for f in range(F):
                gather(f)
            before = Step(-1, -1, -1)
            for u in range(2 * FG, UNITS):
                unit = unit_list(before)[u]
                if on_pool(unit):
                    low_part(before, u, unit)
            run_steps(pool, one_step)

        def block_view(ap):
            return ap.rearrange("p (k d b) -> p d k b", d=D, b=BLK)

        @block.scalar
        def _(act):
            def copy(dst, src):
                return act.activation(dst, src, ACT.Copy)

            def columns_hi(g, dq):
                act.wait_ge(prep_t, g * 4 + (dq + 1))
                copy(block_view(x0_cols[0:F, :])[:, 4 * dq:4 * dq + 4],
                     side[dq % 2][0:F, :].rearrange("p (d k b) -> p d k b", d=4, b=BLK)).then_inc(cols_hi, 1)

            def rows(g, i):
                act.wait_ge(rows_t, g * 2 + (i + 1))
                copy(x0_rows[:, 8 * i:8 * i + 8, :],
                     side[i][:, 0:8 * FS].rearrange("p (k f) -> p k f", f=FS)).then_inc(rows_in, 1)

            def three(step, k):
                act.wait_ge(rep_ready, reps_through(step, k))
                if step.place >= 0:
                    prev = step.back()
                    act.wait_ge(prod, products_through(prev, items_of(prev).index(("B", C0 - 1))))
                copy(x0_three[:, :], rep[bank(k)][:, :]).then_inc(three_in, 1)

            def high_part(step, k, u, unit):
                act.wait_ge(prod, products_through(step, k))
                if step.place >= 0:
                    act.wait_ge(unit_done, units_through(step, u - 4))
                s = slot(u)
                n = 1 if unit[:2] == ("L0", 3) else 2
                copy(z_hi[:, s, 0:n, :], z[:, s, 0:n, :]).then_inc(hi_done, 1)

            def x1_out(step, u):
                act.wait_ge(unit_done, units_through(step, u))
                if step.place >= 1:
                    act.wait_ge(prod, products_through(step.back(), ITEMS - 1))
                copy(x1_rot[:, (step.place + 1) % 2, 0, :], acc0[:, :]).then_inc(x1_in, 1)

            def x2_out(value, b):
                act.wait_ge(unit_done, value * UNITS + (4 + UNITS) if b is not None else 4 + UNITS * value + 2 * FG)
                if not (isinstance(value, int) and value == 0):
                    act.wait_ge(x2_t, value)
                copy(x2_sb[:, :], acc1[b if b is not None else value % 2][:, :]).then_inc(x2_in, 1)

            def x2_rows_out(value, after_top):
                act.wait_ge(x2_t, value + 1)
                if not (isinstance(value, int) and value == 0):
                    act.wait_ge(s_ready, value * NBLK)
                if after_top is not None:
                    act.wait_ge(h2_ready, after_top)
                copy(x2_rows[:, :, :], side[0][:, :].rearrange("p (k m) -> p k m", m=P)).then_inc(x2_rows_in, 1)

            def s_out(value, q, blk, groups_read):
                act.wait_ge(s_ready, value * NBLK + (blk + 1))
                if groups_read is not None:
                    act.wait_ge(r2_ready, groups_read)
                    act.wait_ge(h1_ready, groups_read)
                at = 32 * q + BLK * blk
                copy(s_sb[:, :, at:at + BLK],
                     side[1][:, 0:BLK * FS].rearrange("p (b f) -> p f b", f=FS)).then_inc(s_in, 1)

            def r2_out(g):
                act.wait_ge(r2_ready, g + 1)
                copy(r2_sb[:, :], side[0][:, 0:P]).then_inc(r2_in, 1)

            def h1_out(g):
                act.wait_ge(h1_ready, g + 1)
                for c in range(H1 // P):
                    act.activation(h1_sb[:, c, :], side[1][:, c * P:(c + 1) * P], ACT.Relu,
                                   bias=bt1_sb[:, c:c + 1]).then_inc(h1_in, 1)

            def h2_out(g):
                act.wait_ge(h2_ready, g + 1)
                for c in range(H2 // P):
                    act.activation(h2_sb[:, c, :], side[0][:, c * P:(c + 1) * P], ACT.Relu,
                                   bias=bt2_sb[:, c:c + 1]).then_inc(h2_in, 1)

            def y_out_of(g):
                act.wait_ge(y_ready, g + 1)
                copy(y_sb[:, :], side[1][0:1, 0:P]).then_inc(y_in, 1)

            def one_step(step):
                items = items_of(step)
                last = len(items) - 1
                due = {k: [] for k in range(last + 1)}
                if step.place > 0:
                    tile, q = step.value - 1, (step.q - 1) % TPG
                    due[1].append(lambda: x2_out(tile, (step.place - 1) % 2))
                    at = S_AT[step.q]
                    after_top = step.group if step.q == 1 and step.place > 1 else None
                    due[at[0] + LAG].append(lambda: x2_rows_out(tile, after_top))
                    for i in range(NBLK):
                        read = step.group if step.q == 1 and step.place > 1 else None
                        due[min(at[1 + i] + LAG, last)].append(lambda i=i, read=read: s_out(tile, q, i, read))
                if step.q == 0 and step.place > 0:
                    g = step.group - 1
                    due[L2_AT[-1] + LAG].append(lambda: r2_out(g))
                    due[TOP_AT[0] + LAG].append(lambda: h1_out(g))
                    due[TOP_AT[1] + LAG].append(lambda: h2_out(g))
                    due[min(TOP_AT[2] + LAG, last)].append(lambda: y_out_of(g))
                if step.q == 3 and step.place < TILES - 1:
                    for dq in reversed(range(4)):
                        due[PREP_AT[dq] + LAG].insert(0, lambda dq=dq: columns_hi(step.group + 1, dq))
                    for i in range(2):
                        def rows_after_diag(i=i):
                            act.wait_ge(diag_in, step.value + 1)
                            rows(step.group + 1, i)
                        due[X0D_AT[i] + LAG].append(rows_after_diag)
                if ("B", C0 - 1) in items:
                    k = items.index(("B", C0 - 1))
                    due[min(k + 1, last)].append(lambda: x1_out(step, unit_at(step, k)))
                if step.q == 2:
                    act.wait_ge(rep_ready, reps_through(step.back(), 0))
                    act.wait_ge(cols_lo, step.group * 4 + 4)
                    act.wait_ge(cols_hi, step.group * 4 + 4)
                    copy(x0_last[:, :], x0_cols[:, 3 * COLS:4 * COLS]).then_inc(last_in, 1)
                for k, item in enumerate(items):
                    if item[0] == "A":
                        three(step, k)
                    for i, unit in enumerate(units_of(item)):
                        high_part(step, k, unit_at(step, k) + i, unit)
                    for f in due[k]:
                        f()
                if step.q == 0 and step.place > 0:
                    act.wait_ge(h1_ready, step.group)
                act.wait_ge(r0_done, step.value + 1)
                copy(r0_sb[:, 32 * step.q:32 * step.q + 32], r0_tile[:, step.place % 2, :]).then_inc(r0_in, 1)

            act.wait_ge(weights_in, 80)
            copy(sel[:, :], sel_raw).then_inc(w_hi_done, 1)
            act.wait_ge(w0_sum, 1)
            copy(w0_hi[:, :, :], w0_raw).then_inc(w_hi_done, 1)
            act.wait_ge(w1_in, 16)
            copy(w1_hi[:, :, :], w1_raw[:, :, :]).then_inc(w_hi_done, 1)
            act.wait_ge(blank, 1)
            for dq in range(4):
                columns_hi(0, dq)
            for i in range(2):
                rows(0, i)
            before = Step(-1, -1, -1)
            for k, item in enumerate(items_of(before)):
                if item == ("A", 0):
                    three(before, k)
                elif item is not None:
                    for unit in units_of(item):
                        high_part(before, k, unit_at(before, k), unit)
            act.wait_ge(w_lo_done, 1)
            x1_out(before, UNITS - 1)
            run_steps(act, one_step)
            x2_out(TILES - 1, None)
            x2_rows_out(TILES - 1, None)
            for i in range(NBLK):
                s_out(TILES - 1, TPG - 1, i, None)
            r2_out(GROUPS - 1)
            h1_out(GROUPS - 1)
            h2_out(GROUPS - 1)
            y_out_of(GROUPS - 1)

        @block.vector
        def _(dve):
            def columns_lo(g, dq):
                dve.wait_ge(cols_hi, g * 4 + (dq + 1))
                d = slice(4 * dq, 4 * dq + 4)
                dve.tensor_tensor(block_view(x0_cols[LO:LO + F, :])[:, d],
                                  side[dq % 2][0:F, :].rearrange("p (d k b) -> p d k b", d=4, b=BLK),
                                  block_view(x0_cols[0:F, :].bitcast(F32))[:, d], ALU.subtract).then_inc(cols_lo, 1)

            def product(step, k, item):
                kind, n = item
                u = unit_at(step, k)
                if kind == "L1" or n % 2 == 0:
                    for i in range(2 if kind == "L1" else 1):
                        if step.place >= 0:
                            wait_low(dve, step, u + i - 4)
                dve.wait_ge(rep_ready, reps_through(step, k))
                b = bank(k)
                if kind == "L1":
                    if n == 0:
                        dve.wait_ge(x1_turned, step.value * 96 + 96)
                    s = slot(u)
                    dve.tensor_tensor(z[:, s:s + 2, :, :].rearrange("p a c n -> p (a c) n"),
                                      rep[b][:, None, :].to_broadcast([P, ROT, COLS]),
                                      x1_rot[:, step.place % 2, :, :], ALU.mult).then_inc(prod, 1)
                else:
                    if n == 0:
                        dve.wait_ge(three_in, step.value + 2)
                    dve.tensor_tensor(z[:, slot(u), n % 2, :], rep[b][:, :], x0_three[:, :],
                                      ALU.mult).then_inc(prod, 1)

            def low_parts(step, k):
                if k < 0:
                    step = step.back()
                    k += len(items_of(step))
                item = items_of(step)[k]
                for i, unit in enumerate(units_of(item)):
                    if unit is None or on_pool(unit):
                        continue
                    u = unit_at(step, k) + i
                    dve.wait_ge(hi_done, units_through(step, u))
                    if step.place >= 0:
                        dve.wait_ge(unit_done, units_through(step, u - 4))
                    s = slot(u)
                    n = 1 if unit[:2] == ("L0", 3) else 2
                    dve.tensor_tensor(z_lo[:, s, 0:n, :], z[:, s, 0:n, :], z_hi[:, s, 0:n, :].bitcast(F32),
                                      ALU.subtract).then_inc(lo_dve, 1)

            def spread_rows(step):
                dve.wait_ge(rows_in, step.group * 2 + 2)
                if step.place > 0:
                    dve.wait_ge(s_ready, step.value * NBLK)
                q = step.q
                dve.tensor_tensor(diag[:, :, :, :],
                                  x0_rows[:, 4 * q:4 * q + 4, None, :].to_broadcast([P, NBLK, BLK, FS]),
                                  mask_sb[:, None, :, None].to_broadcast([P, NBLK, BLK, FS]),
                                  ALU.mult).then_inc(diag_in, 1)

            def sum_x1(step):
                dve.wait_ge(x1_in, step.value + 2)
                if step.place >= 1:
                    dve.wait_ge(r0_in, step.value)
                b = (step.place + 1) % 2
                dve.tensor_reduce(r0_tile[:, b, :].rearrange("p (k b) -> p k b", b=BLK),
                                  x1_rot[:, b, 0, :].rearrange("p (k d b) -> p k b d", d=D, b=BLK),
                                  AX_X, ALU.add).then_inc(r0_done, 1)

            def one_step(step):
                items = items_of(step)
                last = len(items) - 1
                due = {k: [] for k in range(last + 1)}
                due[min(S_AT[step.q][4] + LAG, last)].append(lambda: spread_rows(step))
                if step.q == 3 and step.place < TILES - 1:
                    for dq in range(4):
                        due[PREP_AT[dq] + LAG].append(lambda dq=dq: columns_lo(step.group + 1, dq))
                if ("B", C0 - 1) in items:
                    due[min(items.index(("B", C0 - 1)) + LAG + 1, last)].append(lambda: sum_x1(step))
                for k, item in enumerate(items):
                    if item[0] != "A":
                        product(step, k, item)
                    if step.place > 0 or k > 0:
                        low_parts(step, k - 1)
                    for f in due[k]:
                        f()

            dve.memset(x0_cols[32:LO, :].bitcast(F32), 1.0).then_inc(blank, 1)
            dve.wait_ge(weights_in, 80)
            dve.tensor_tensor(w0_raw, w0a_raw, w0b_raw, ALU.add).then_inc(w0_sum, 1)
            dve.wait_ge(w_hi_done, 2)
            dve.tensor_tensor(w0_lo[:, :, :], w0_raw, w0_hi[:, :, :].bitcast(F32), ALU.subtract).then_inc(w_lo_done, 1)
            dve.wait_ge(w_hi_done, 3)
            dve.tensor_tensor(w1_lo[:, :, :], w1_raw[:, :, :], w1_hi[:, :, :].bitcast(F32),
                              ALU.subtract).then_inc(w_lo_done, 1)
            for dq in range(4):
                columns_lo(0, dq)
            before = Step(-1, -1, -1)
            for k, item in enumerate(items_of(before)):
                if item is not None:
                    if item[0] == "B":
                        product(before, k, item)
                    low_parts(before, k - 1)
            low_parts(before, ITEMS - 1)
            sum_x1(before)
            run_steps(dve, one_step)
            low_parts(Step(TILES - 1, TILES - 1, None), FG - 1)

        @block.tensor
        def _(pe):
            def columns_t(g, dq):
                for i in range(4):
                    mm = pe.matmul(side[dq % 2][0:F, i * P:(i + 1) * P], emb[:, :, 4 * dq + i], ident[:, :],
                                   start=True, stop=True)
                mm.then_inc(prep_t, 1)

            def rows_of(g, i):
                pe.wait_ge(cols_hi, g * 4 + 4)
                pe.wait_ge(cols_lo, g * 4 + 4)
                for k in range(8):
                    at = (8 * i + k) * P
                    mm = pe.matmul(side[i][:, k * FS:(k + 1) * FS], x0_cols[:, at:at + P], sel[:, NSEL * P:SEL_COLS],
                                   start=True, stop=True)
                mm.then_inc(rows_t, 1)

            def replicate(step, k):
                n_items = len(items_of(step))
                if k >= n_items:
                    if step.place == TILES - 1:
                        return
                    step = Step(step.value + 1, step.place + 1, None)
                    k -= n_items
                kind, n = items_of(step)[k]
                prev, j = (step, k - 3) if k >= 3 else (step.back(), k - 3 + ITEMS)
                old = items_of(prev)[j]
                if old is not None:
                    if old[0] == "A":
                        pe.wait_ge(three_in, prev.value + 2)
                    else:
                        pe.wait_ge(prod, products_through(prev, j))
                q = step.q if kind == "L1" else (step.q + 1) % TPG
                if kind == "A" and q == 0:
                    pe.wait_ge(cols_hi, step.group * 4 + 8)
                    pe.wait_ge(cols_lo, step.group * 4 + 8)
                cols = x0_last[:, :] if kind == "L1" and q == 3 else x0_cols[:, q * COLS:(q + 1) * COLS]
                which = {"L1": SEL_REP + n, "A": SEL_A, "B": SEL_B + n}[kind]
                pe.matmul(rep[bank(k)][:, :], sel[:, which * P:(which + 1) * P], cols,
                          start=True, stop=True).then_inc(rep_ready, 1)

            def contract(step, u, unit):
                kind, n, half = unit
                s = slot(u)
                if kind == "L1":
                    acc, hi, lo, first = acc1[step.place % 2], w1_hi, w1_lo, ROT * n + 2 * half
                    chunks, opens, closes = 2, first == 0, (n, half) == (FG - 1, 1)
                    if opens and step.place >= 1:
                        pe.wait_ge(x2_in, step.value - 1)
                else:
                    acc, hi, lo, first = acc0, w0_hi, w0_lo, 2 * n
                    chunks, opens, closes = min(2, C0 - first), n == 0, n == 3
                    if opens and step.place >= 0:
                        pe.wait_ge(x1_in, step.value + 1)
                pe.wait_ge(hi_done, units_through(step, u))
                for i in range(chunks):
                    pe.matmul(acc[:, :], hi[:, first + i, :], z_hi[:, s, i, :], start=opens and i == 0, stop=False)
                    pe.matmul(acc[:, :], lo[:, first + i, :], z_hi[:, s, i, :], start=False, stop=False)
                wait_low(pe, step, u)
                for i in range(chunks):
                    mm = pe.matmul(acc[:, :], hi[:, first + i, :], z_lo[:, s, i, :], start=False,
                                   stop=closes and i == chunks - 1)
                mm.then_inc(unit_done, 1)

            def x2_transpose(value):
                pe.wait_ge(x2_in, value + 1)
                for i in range(NBLK):
                    mm = pe.transpose(side[0][:, i * P:(i + 1) * P], x2_sb[:, i * P:(i + 1) * P], ident[:, :])
                mm.then_inc(x2_t, 1)

            def s_block(value, i):
                if i == 0:
                    pe.wait_ge(x2_rows_in, value + 1)
                    pe.wait_ge(diag_in, value + 1)
                else:
                    pe.wait_ge(s_in, value * NBLK + i)
                pe.matmul(side[1][:, 0:BLK * FS], x2_rows[:, i, :], diag[:, i, :, :].rearrange("p b f -> p (b f)"),
                          start=True, stop=True).then_inc(s_ready, 1)

            def layer2(g, i):
                if i == 0:
                    pe.wait_ge(s_in, g * (TPG * NBLK) + TPG * NBLK)
                    pe.wait_ge(top_in, 112)
                for f in range(L2_CUT[i], L2_CUT[i + 1]):
                    mm = pe.matmul(side[0][:, 0:P], w2_sb[:, f, :], s_sb[:, f, :], start=f == 0, stop=f == F - 1)
                if i == 2:
                    mm.then_inc(r2_ready, 1)

            def top1(g):
                pe.wait_ge(r2_in, g + 1)
                pe.wait_ge(r0_in, g * TPG + TPG)
                pe.wait_ge(dense_in, g * 16 + 16)
                for c in range(H1 // P):
                    cut = slice(c * P, (c + 1) * P)
                    for i, x in enumerate((r0_sb[:, :], s_sb[:, F, :], r2_sb[:, :])):
                        pe.matmul(side[1][:, cut], wt1_sb[:, i, cut], x, start=i == 0, stop=False)
                    mm = pe.matmul(side[1][:, cut], wt1_sb[0:16, 3, cut], dense_sb[:, :], start=False, stop=True)
                mm.then_inc(h1_ready, 1)

            def top2(g):
                pe.wait_ge(h1_in, g * 4 + 4)
                for c in range(H2 // P):
                    cut = slice(c * P, (c + 1) * P)
                    for i in range(H1 // P):
                        mm = pe.matmul(side[0][:, cut], wt2_sb[:, i, cut], h1_sb[:, i, :], start=i == 0, stop=i == 3)
                mm.then_inc(h2_ready, 1)

            def top3(g):
                pe.wait_ge(h2_in, g * 2 + 2)
                for i in range(H2 // P):
                    mm = pe.matmul(side[1][0:1, 0:P], wt3_sb[:, i:i + 1], h2_sb[:, i, :], start=i == 0, stop=i == 1)
                mm.then_inc(y_ready, 1)

            def one_step(step):
                items = items_of(step)
                jobs = {k: [] for k in range(len(items))}
                if step.q == 3 and step.place < TILES - 1:
                    g = step.group + 1

                    def prepare(dq):
                        if dq == 0:
                            pe.wait_ge(gathered, g * (16 * F) + 16 * F)
                            pe.wait_ge(x2_rows_in, step.value - 1)
                        elif dq == 1:
                            pe.wait_ge(s_in, step.value * NBLK - NBLK)
                        else:
                            pe.wait_ge(cols_lo, g * 4 + (dq - 1))
                        columns_t(g, dq)

                    for dq in range(4):
                        jobs[PREP_AT[dq]].append(lambda dq=dq: prepare(dq))

                    def tile_rows(i):
                        if i == 0:
                            pe.wait_ge(x2_rows_in, step.value)
                        else:
                            pe.wait_ge(s_in, step.value * NBLK)
                        rows_of(g, i)

                    for i in range(2):
                        jobs[X0D_AT[i]].append(lambda i=i: tile_rows(i))
                if step.place > 0:
                    tile = step.value - 1
                    at = S_AT[step.q]

                    def turn():
                        if step.q == 3 and step.place < TILES - 1:
                            pe.wait_ge(cols_lo, step.group * 4 + 7)
                        elif step.q == 1 and step.place > 1:
                            pe.wait_ge(h2_in, step.group * 2)
                        elif step.q == 0:
                            pe.wait_ge(rows_in, step.group * 2 + 2)
                        x2_transpose(tile)

                    def first_block():
                        if step.q == 3 and step.place < TILES - 1:
                            pe.wait_ge(cols_lo, step.group * 4 + 8)
                        elif step.q == 1 and step.place > 1:
                            pe.wait_ge(y_in, step.group)
                        s_block(tile, 0)

                    jobs[at[0]].append(turn)
                    jobs[at[1]].append(first_block)
                    for i in range(1, NBLK):
                        jobs[at[1 + i]].append(lambda i=i: s_block(tile, i))
                if step.q == 0 and step.place > 0:
                    g0 = step.group - 1
                    for i in range(3):
                        jobs[L2_AT[i]].append(lambda i=i: layer2(g0, i))
                    for k, f in zip(TOP_AT, (top1, top2, top3)):
                        jobs[k].append(lambda f=f: f(g0))
                if step.q == 2:
                    jobs[len(items) - AHEAD - 1].append(lambda: pe.wait_ge(last_in, step.group + 1))
                for k, item in enumerate(items):
                    replicate(step, k + AHEAD)
                    for i, unit in enumerate(units_of(item)):
                        contract(step, unit_at(step, k) + i, unit)
                    for job in jobs[k]:
                        job()

            pe.wait_ge(weights_in, 80)
            pe.wait_ge(gathered, 16 * F)
            for dq in range(4):
                if dq > 1:
                    pe.wait_ge(cols_lo, dq - 1)
                columns_t(0, dq)
            pe.wait_ge(cols_lo, 4)
            pe.wait_ge(w_hi_done, 2)
            rows_of(0, 0)
            rows_of(0, 1)
            before = Step(-1, -1, -1)
            for k in range(FG, FG + AHEAD):
                replicate(before, k)
            pe.wait_ge(w_lo_done, 2)
            for k in range(FG, ITEMS):
                if k + AHEAD < ITEMS + 3:
                    replicate(before, k + AHEAD)
                for unit in units_of(items_of(before)[k]):
                    contract(before, unit_at(before, k), unit)
            replicate(before, ITEMS + 3)
            run_steps(pe, one_step)
            x2_transpose(TILES - 1)
            for i in range(NBLK):
                s_block(TILES - 1, i)
            for i in range(3):
                layer2(GROUPS - 1, i)
            top1(GROUPS - 1)
            top2(GROUPS - 1)
            top3(GROUPS - 1)


def selector_matrices():
    s = np.zeros((F + 1, SEL_COLS), np.float32)
    for g in range(FG):
        for j in range(4):
            if 4 * g + j < F:
                s[4 * g + j, (SEL_REP + g) * P + 32 * j:(SEL_REP + g) * P + 32 * j + 32] = 1.0
    for r in range(3):
        for f in range(F):
            s[f, SEL_A * P + F * r + f] = 1.0
    for c in range(C0):
        for r in range(3):
            if 3 * c + r <= F // 2:
                for f in range(F):
                    s[(f + 3 * c + r) % F, (SEL_B + c) * P + F * r + f] = 1.0
    for f in range(FS):
        s[f, NSEL * P + f] = 1.0
    full = np.zeros((P, SEL_COLS), np.float32)
    full[0:F + 1] = s
    full[LO:LO + F] = s[0:F]
    return full


def kernel(**inputs):
    import concourse.bacc as bacc
    from concourse.bass_utils import run_bass_kernel_spmd

    f0 = np.asarray(inputs["L0_rec_f0"]).reshape(F, F, M)
    f1 = np.asarray(inputs["L0_rec_f1"]).reshape(F, M, M)
    f2 = np.asarray(inputs["L0_rec_f2"]).reshape(F, M, M)
    w0a = np.zeros((P, C0, M), np.float32)
    w0b = np.zeros((P, C0, M), np.float32)
    for c in range(C0):
        for r in range(3):
            shift = 3 * c + r
            if shift <= F // 2:
                f = np.arange(F)
                w0a[F * r:F * r + F, c] = f0[f, (f + shift) % F]
                if shift:
                    w0b[F * r:F * r + F, c] = f0[(f + shift) % F, f]
    w1 = np.zeros((P, FG * ROT, M), np.float32)
    for g in range(FG):
        for j in range(4):
            if 4 * g + j < F:
                for r in range(ROT):
                    at = 32 * ((j + r) % 4)
                    w1[32 * j:32 * j + 32, ROT * g + r] = f1[4 * g + j, at:at + 32]
    position = np.arange(P)
    mask8 = (position[:, None] % BLK == np.arange(BLK)[None, :]).astype(np.float32)

    arrays = {
        "ids": np.asarray(inputs["ids"]),
        **{f"tbl_{f}": np.asarray(inputs[f"tbl_{f}"]) for f in range(F)},
        "w0a": w0a, "w0b": w0b, "w1": w1,
        "w2": np.ascontiguousarray(f2.transpose(1, 0, 2)),
        "W_top1": np.asarray(inputs["W_top1"]),
        "b_top1": np.ascontiguousarray(np.asarray(inputs["b_top1"]).reshape(H1 // P, P).T),
        "W_top2": np.asarray(inputs["W_top2"]),
        "b_top2": np.ascontiguousarray(np.asarray(inputs["b_top2"]).reshape(H2 // P, P).T),
        "W_top3": np.ascontiguousarray(np.asarray(inputs["W_top3"]).reshape(H2 // P, P).T),
        "dense_t": np.ascontiguousarray(np.asarray(inputs["dense_ctx"]).T),
        "selectors": selector_matrices(),
        "identity": np.eye(P, dtype=np.float32),
        "mask8": mask8,
    }
    nc = bacc.Bacc("TRN2", target_bir_lowering=False, num_devices=1)
    ap = {name: nc.dram_tensor(f"in_{name}_dram", a.shape, mybir.dt.from_np(a.dtype), kind="ExternalInput").ap()
          for name, a in arrays.items()}
    y = nc.dram_tensor("out_0_dram", (B, 1), F32, kind="ExternalOutput").ap()
    cross_network(nc, ap["ids"], [ap[f"tbl_{f}"] for f in range(F)], ap["w0a"], ap["w0b"], ap["w1"], ap["w2"],
                  ap["W_top1"], ap["b_top1"], ap["W_top2"], ap["b_top2"], ap["W_top3"], ap["dense_t"],
                  ap["selectors"], ap["identity"], ap["mask8"], y)
    r = run_bass_kernel_spmd(nc, [{f"in_{name}_dram": a for name, a in arrays.items()}], core_ids=[0])
    return r.results[0]["out_0_dram"]
```

```python
from contextlib import ExitStack

import numpy as np

import concourse.bass as bass
from concourse import mybir

F32 = mybir.dt.float32
F32R = mybir.dt.float32r
I32 = mybir.dt.int32
ALU = mybir.AluOpType
ACT = mybir.ActivationFunctionType
AX_X = mybir.AxisListType.X

B = 512
F = 39
D = 16
M = 128
P = 128
FEATURES = 3 * M + 16
H1, H2 = 512, 256

COLS = 512
BLK = 8
GROUPS = B // P
TPG = 4
TILES = GROUPS * TPG
NBLK = COLS // P
LO = 64
KX = LO + F
FG = 10
ROT = 4
C0 = 7
FS = F + 1

SEL_REP = 0
SEL_A = FG
SEL_B = FG + 1
NSEL = FG + 1 + C0
SEL_COLS = NSEL * P + FS

UNITS = FG + 2
SPLIT = 3
WHOLE0 = 3
ITEMS = FG + 1 + C0
AHEAD = 4


def items_of(step):
    cross = [("L1", g) for g in range(FG)]
    if step.place == TILES - 1:
        return cross
    if step.place < 0:
        return [None] * FG + [("A", 0)] + [("B", c) for c in range(C0)]
    first = L0_AT[step.q]
    return cross[:first] + [("A", 0)] + [("B", c) for c in range(C0)] + cross[first:]


def unit_of(step, k):
    items = items_of(step)
    kind, n = items[k]
    if kind == "B":
        at = items.index(("A", 0))
        return at + (0 if n <= WHOLE0 else 1)
    at = items.index(("A", 0)) if ("A", 0) in items else len(items)
    return k if k < at else k - ITEMS + UNITS


def splits_at(item):
    return item is not None and (item[0] == "L1" or item in (("B", 2), ("B", C0 - 1)))


def contracts_at(item):
    return item is not None and (item[0] == "L1" or item in (("B", WHOLE0), ("B", C0 - 1)))


class Step:

    def __init__(self, value, place, group):
        self.value, self.place, self.group = value, place, group

    @property
    def q(self):
        return self.place % TPG

    def back(self, n=1):
        return Step(self.value - n, self.place - n, None)


def units_through(step, u):
    return step.value * UNITS + (2 + u + 1)


def reps_through(step, k):
    return step.value * ITEMS + (1 + C0 + k + 1)


def products_through(step, k, part=1):
    count = {"L1": 2, "A": 0, "B": 1}
    names = items_of(step)[:k + 1]
    here = sum(count[it[0]] for it in names if it is not None)
    if names[-1] is not None and names[-1][0] == "L1" and part == 0:
        here -= 1
    if step.place < 0:
        return here
    return step.value * (2 * FG + C0) + (C0 + here)


def fields_before(q, u):
    order = (3, 0, 1, 2)
    return sum(sum(GATHER_AT[x]) for x in order[:order.index(q)]) + sum(GATHER_AT[q][:u])


def ring(u):
    return u % 3


def bank(k):
    return (1 + C0 + k) % 3


S_AT_LAST = (1, 2, 3, 4, 5)
L0_AT = (4, 4, 4, 4)
S_AT = {0: (1, 3, 4, 5, 6), 1: (1, 3, 5, 7, 9), 2: (1, 3, 5, 7, 9), 3: (1, 3, 5, 7, 9)}
L2_AT = (8, 10, 12)
TOP_AT = (14, 16, 17)
PREP_AT = (13, 13, 14, 15)
X0D_AT = (13, 14)
L2_CUT = (0, 13, 26, F)
DIAG_AT = {0: 13, 1: 13, 2: 13, 3: 13}
LAG = 2
X1_LAG = 1
WARM = (12, 9, 34)
GATHER_AT = {
    3: (0, 0, 1, 0, 2, 1, 1, 1, 1, 1, 1, 0),
    0: (1, 1, 1, 1, 2, 2, 1, 2, 2, 2, 2, 1),
    1: (0, 1, 1, 0, 1, 1, 1, 1, 0, 1, 1, 0),
    2: (0, 1, 0, 1, 1, 1, 0, 0, 0, 0, 0, 0),
}
LAST_GATHER = 2 * TPG - 2


def cross_network(nc, ids, tables, w0a, w0b, w1, w1_w, w2, wt1, bt1, wt2, bt2, wt3, dense_t, selectors, identity, mask8, out):
    with ExitStack() as ctx:
        def sb(name, shape, dt=F32):
            return ctx.enter_context(nc.sbuf_tensor(name, shape, dt))

        def ps(name, shape):
            return ctx.enter_context(nc.psum_tensor(name, shape, F32))

        def sem(name):
            return ctx.enter_context(nc.semaphore(name))

        w1_hi = sb("w1_hi", [P, FG * SPLIT, M], F32R)
        w1_lo = sb("w1_lo", [P, FG * SPLIT, M], F32R)
        w1_whole = sb("w1_whole", [P, FG, M])
        w0_hi = sb("w0_hi", [P, C0, M], F32R)
        w0_lo = sb("w0_lo", [P, C0, M], F32R)
        w0_whole = sb("w0_whole", [P, M])
        w2_sb = sb("w2_sb", [P, F, M])
        wt1_sb = sb("wt1_sb", [P, 4, H1])
        wt2_sb = sb("wt2_sb", [P, H1 // P, H2])
        wt3_sb = sb("wt3_sb", [P, H2 // P])
        bt1_sb = sb("bt1_sb", [P, H1 // P])
        bt2_sb = sb("bt2_sb", [P, H2 // P])
        sel = sb("sel", [KX, SEL_COLS], F32R)
        ident = sb("ident", [P, P])
        mask_sb = sb("mask_sb", [P, BLK])
        tick = sb("tick", [1, 1])
        ids_now = sb("ids_now", [P, F], I32)
        emb = sb("emb", [P, F, D])
        x0_cols = sb("x0_cols", [KX, TPG * COLS], F32R)
        x0_last = sb("x0_last", [KX, COLS], F32R)
        x0_three = sb("x0_three", [P, COLS])
        x0_rows = sb("x0_rows", [P, TPG * NBLK, FS])
        z = sb("z", [P, 2, SPLIT, COLS])
        z_whole = sb("z_whole", [P, 3, COLS])
        z_hi = sb("z_hi", [P, 3, SPLIT, COLS], F32R)
        z_lo = sb("z_lo", [P, 3, SPLIT, COLS], F32R)
        x1_rot = sb("x1_rot", [P, 2, ROT, COLS])
        x2_sb = sb("x2_sb", [P, COLS])
        x2_rows = sb("x2_rows", [P, NBLK, P])
        diag = sb("diag", [P, NBLK, BLK, FS])
        s_sb = sb("s_sb", [P, FS, P])
        r0_tile = sb("r0_tile", [P, 2, NBLK * BLK])
        r0_sb = sb("r0_sb", [P, P])
        r2_sb = sb("r2_sb", [P, P])
        dense_sb = sb("dense_sb", [16, P])
        h1_sb = x2_rows
        h2_sb = sb("h2_sb", [P, H2 // P, P])
        y_sb = sb("y_sb", [1, P])

        w1_raw = s_sb[:, 0:FG * SPLIT, :]
        zf = z[:, :, :, :].rearrange("p a b n -> p (a b n)")
        w0a_raw = x1_rot[:, 0, :, :].rearrange("p a n -> p (a n)")[:, 0:C0 * M].rearrange("p (c m) -> p c m", c=C0)
        w0b_raw = x1_rot[:, 0, :, :].rearrange("p a n -> p (a n)")[:, C0 * M:2 * C0 * M].rearrange("p (c m) -> p c m", c=C0)
        w0_raw = x1_rot[:, 1, :, :].rearrange("p a n -> p (a n)")[:, 0:C0 * M].rearrange("p (c m) -> p c m", c=C0)
        sel_raw = zf[0:KX, 0:SEL_COLS]

        rep = [ps(f"rep{i}", [P, COLS]) for i in range(3)]
        acc0 = ps("acc0", [P, COLS])
        acc1 = [ps(f"acc1_{i}", [P, COLS]) for i in range(2)]
        side = [ps("side_t", [P, COLS]), ps("side_s", [P, COLS])]

        ids_in = sem("ids_in")
        weights_in = sem("weights_in")
        w1_in = sem("w1_in")
        nearly = sem("nearly")
        top_in = sem("top_in")
        dense_in = sem("dense_in")
        blank = sem("blank")
        w0_sum = sem("w0_sum")
        w_hi_done = sem("w_hi_done")
        w_lo_done = sem("w_lo_done")
        gathered = sem("gathered")
        prep_t = sem("prep_t")
        cols_hi = sem("cols_hi")
        cols_lo = sem("cols_lo")
        rows_t = sem("rows_t")
        rows_in = sem("rows_in")
        last_in = sem("last_in")
        rep_ready = sem("rep_ready")
        three_in = sem("three_in")
        prod = sem("prod")
        hi_two = sem("hi_two")
        hi_third = sem("hi_third")
        lo_pool = sem("lo_pool")
        lo_dve = sem("lo_dve")
        unit_done = sem("unit_done")
        x1_in = sem("x1_in")
        x1_turned = sem("x1_turned")
        r0_done = sem("r0_done")
        r0_in = sem("r0_in")
        x2_in = sem("x2_in")
        x2_t = sem("x2_t")
        x2_rows_in = sem("x2_rows_in")
        diag_in = sem("diag_in")
        s_ready = sem("s_ready")
        s_in = sem("s_in")
        r2_ready = sem("r2_ready")
        r2_in = sem("r2_in")
        h1_ready = sem("h1_ready")
        h1_in = sem("h1_in")
        h2_ready = sem("h2_ready")
        h2_in = sem("h2_in")
        y_ready = sem("y_ready")
        y_in = sem("y_in")
        y_out = sem("y_out")

        def prep_bank(g, dq):
            first = isinstance(g, int) and g == 0
            return (side + acc1)[dq] if first else side[dq % 2]

        def turn_quadrants(eng, b, r):
            cut = P - 32 * r
            eng.dma_start(x1_rot[0:cut, b, r, :], x1_rot[32 * r:P, b, 0, :]).then_inc(x1_turned, 16)
            eng.dma_start(x1_rot[cut:P, b, r, :], x1_rot[0:32 * r, b, 0, :]).then_inc(x1_turned, 16)

        block = ctx.enter_context(nc.Block())

        def run_steps(eng, step_of):
            for n in range(TPG - 1):
                step_of(Step(n, n, 0))
            with eng.Fori(0, GROUPS - 2) as g:
                for n in range(TPG - 1, 2 * TPG - 1):
                    step_of(Step(g * TPG + n, n, g + n // TPG))
            for n in range(TILES - TPG - 1, TILES):
                step_of(Step(n, n, n // TPG))

        def wait_low(eng, step, u):
            eng.wait_ge(lo_pool, units_through(step, u))
            eng.wait_ge(lo_dve, units_through(step, u))

        @block.sync
        def _(sp):
            def turn_x1(value, b, rotations=range(1, ROT)):
                sp.wait_ge(x1_in, value + 1)
                for r in rotations:
                    turn_quadrants(sp, b, r)

            def store_y(g):
                sp.wait_ge(y_in, g + 1)
                sp.dma_start(out[bass.ds(g * P, P), :].rearrange("b o -> o b"), y_sb[:, :]).then_inc(y_out, 16)

            def load_dense(g):
                sp.dma_start(dense_sb[:, :], dense_t[:, bass.ds(g * P, P)]).then_inc(dense_in, 16)

            def load_ids(g):
                sp.dma_start(ids_now[:, :], ids[bass.ds(g * P, P), :]).then_inc(ids_in, 16)

            load_ids(0)
            sp.dma_start(sel_raw, selectors[0:KX, :]).then_inc(weights_in, 16)
            sp.dma_start(w0a_raw, w0a).then_inc(weights_in, 16)
            sp.dma_start(w0b_raw, w0b).then_inc(weights_in, 16)
            sp.dma_start(ident[:, :], identity).then_inc(weights_in, 16)
            sp.dma_start(mask_sb[:, :], mask8).then_inc(weights_in, 16)
            sp.dma_start(w1_raw, w1).then_inc(w1_in, 16)
            sp.dma_start(w1_whole[:, :, :], w1_w).then_inc(top_in, 16)
            sp.dma_start(w2_sb[:, :, :], w2).then_inc(top_in, 16)
            sp.dma_start(wt1_sb[:, 0:3, :], wt1[0:3 * P, :].rearrange("(c p) n -> p c n", p=P)).then_inc(top_in, 16)
            sp.dma_start(wt1_sb[0:16, 3, :], wt1[3 * P:FEATURES, :]).then_inc(top_in, 16)
            sp.dma_start(wt2_sb[:, :, :], wt2.rearrange("(c p) n -> p c n", p=P)).then_inc(top_in, 16)
            sp.dma_start(wt3_sb[:, :], wt3).then_inc(top_in, 16)
            sp.dma_start(bt1_sb[:, :], bt1).then_inc(top_in, 16)
            sp.dma_start(bt2_sb[:, :], bt2).then_inc(top_in, 16)
            load_dense(0)
            sp.wait_ge(gathered, 16 * F)
            load_ids(1)
            turn_x1(0, 0, (3, 2))

            def one_step(step):
                if step.q == 3 and step.place <= LAST_GATHER:
                    sp.wait_ge(gathered, step.group * (16 * F) + 32 * F)
                    load_ids(step.group + 2)
                if step.place < TILES - 1:
                    turn_x1(step.value + 1, (step.place + 1) % 2)
                if step.q == 0 and step.place > 0:
                    store_y(step.group - 1)
                    sp.wait_ge(y_out, step.group * 16)
                    load_dense(step.group)

            run_steps(sp, one_step)
            store_y(GROUPS - 1)
            sp.wait_ge(y_out, 16 * GROUPS)

        @block.gpsimd
        def _(pool):
            def gather(f):
                pool.indirect_dma_start(
                    out=emb[:, f, :], out_offset=None, in_=tables[f][:, :],
                    in_offset=bass.IndirectOffsetOnAxis(ap=ids_now[:, f:f + 1], axis=0),
                ).then_inc(gathered, 16)

            def low_part(step, u):
                pool.wait_ge(hi_two, units_through(step, u))
                if step.place >= 0 and not (step.place == 0 and u == 0):
                    pool.wait_ge(unit_done, units_through(step, u - 3))
                pool.tensor_tensor(z_lo[:, ring(u), 0:2, :], z[:, u % 2, 0:2, :], z_hi[:, ring(u), 0:2, :].bitcast(F32),
                                   ALU.subtract).then_inc(lo_pool, 1)

            def one_step(step):
                counts = GATHER_AT[step.q] if step.place <= LAST_GATHER else [0] * UNITS
                for u in range(FG if step.place == TILES - 1 else UNITS):
                    if counts[u] and step.q == 3 and not any(counts[:u]):
                        pool.wait_ge(prep_t, step.group * 4 + 8)
                        pool.wait_ge(ids_in, step.group * 16 + 48)
                    low_part(step, u)
                    for f in range(fields_before(step.q, u), fields_before(step.q, u + 1)):
                        if counts[u]:
                            gather(f)

            pool.wait_ge(ids_in, 16)
            for f in range(F):
                if f == F - 5:
                    pool.memset(tick[:, :], 0.0).then_inc(nearly, 1)
                gather(f)
            before = Step(-1, -1, -1)
            for u in range(FG, UNITS):
                low_part(before, u)
            pool.wait_ge(prep_t, 4)
            pool.wait_ge(ids_in, 32)
            for f in range(sum(GATHER_AT[3])):
                gather(f)
            run_steps(pool, one_step)

        def block_view(ap):
            return ap.rearrange("p (k d b) -> p d k b", d=D, b=BLK)

        @block.scalar
        def _(act):
            def copy(dst, src):
                return act.activation(dst, src, ACT.Copy)

            def columns_hi(g, dq):
                act.wait_ge(prep_t, g * 4 + (dq + 1))
                copy(block_view(x0_cols[0:F, :])[:, 4 * dq:4 * dq + 4],
                     prep_bank(g, dq)[0:F, :].rearrange("p (d k b) -> p d k b", d=4, b=BLK)).then_inc(cols_hi, 1)

            def rows(g, i):
                act.wait_ge(rows_t, g * 2 + (i + 1))
                copy(x0_rows[:, 8 * i:8 * i + 8, :],
                     side[i][:, 0:8 * FS].rearrange("p (k f) -> p k f", f=FS)).then_inc(rows_in, 1)

            def three(step, k):
                act.wait_ge(rep_ready, reps_through(step, k))
                if step.place >= 0:
                    prev = step.back()
                    act.wait_ge(prod, products_through(prev, items_of(prev).index(("B", C0 - 1))))
                copy(x0_three[:, :], rep[bank(k)][:, :]).then_inc(three_in, 1)

            def high_part(step, k):
                u = unit_of(step, k)
                act.wait_ge(prod, products_through(step, k))
                if step.place >= 0 and not (step.place == 0 and u == 0):
                    act.wait_ge(unit_done, units_through(step, u - 3))
                copy(z_hi[:, ring(u), 0:2, :], z[:, u % 2, 0:2, :]).then_inc(hi_two, 1)
                copy(z_hi[:, ring(u), 2, :], z[:, u % 2, 2, :]).then_inc(hi_third, 1)

            def x1_out(step, u):
                act.wait_ge(unit_done, units_through(step, u))
                if step.place >= 1:
                    act.wait_ge(prod, products_through(step.back(), ITEMS - 1))
                copy(x1_rot[:, (step.place + 1) % 2, 0, :], acc0[:, :]).then_inc(x1_in, 1)

            def x2_out(value, b):
                act.wait_ge(unit_done, value * UNITS + (2 + UNITS) if b is not None else 2 + UNITS * value + FG)
                if not (isinstance(value, int) and value == 0):
                    act.wait_ge(x2_t, value)
                copy(x2_sb[:, :], acc1[b if b is not None else value % 2][:, :]).then_inc(x2_in, 1)

            def x2_rows_out(value, after_top):
                act.wait_ge(x2_t, value + 1)
                if not (isinstance(value, int) and value == 0):
                    act.wait_ge(s_ready, value * NBLK)
                if after_top is not None:
                    act.wait_ge(h2_ready, after_top)
                copy(x2_rows[:, :, :], side[0][:, :].rearrange("p (k m) -> p k m", m=P)).then_inc(x2_rows_in, 1)

            def s_out(value, q, blk, groups_read):
                act.wait_ge(s_ready, value * NBLK + (blk + 1))
                if groups_read is not None:
                    act.wait_ge(r2_ready, groups_read)
                    act.wait_ge(h1_ready, groups_read)
                at = 32 * q + BLK * blk
                copy(s_sb[:, :, at:at + BLK],
                     side[(blk + 1) % 2][:, 0:BLK * FS].rearrange("p (b f) -> p f b", f=FS)).then_inc(s_in, 1)

            def r2_out(g):
                act.wait_ge(r2_ready, g + 1)
                copy(r2_sb[:, :], side[0][:, 0:P]).then_inc(r2_in, 1)

            def h1_out(g):
                act.wait_ge(h1_ready, g + 1)
                for c in range(H1 // P):
                    act.activation(h1_sb[:, c, :], side[1][:, c * P:(c + 1) * P], ACT.Relu,
                                   bias=bt1_sb[:, c:c + 1]).then_inc(h1_in, 1)

            def h2_out(g):
                act.wait_ge(h2_ready, g + 1)
                for c in range(H2 // P):
                    act.activation(h2_sb[:, c, :], side[0][:, c * P:(c + 1) * P], ACT.Relu,
                                   bias=bt2_sb[:, c:c + 1]).then_inc(h2_in, 1)

            def y_out_of(g):
                act.wait_ge(y_ready, g + 1)
                copy(y_sb[:, :], side[1][0:1, 0:P]).then_inc(y_in, 1)

            def one_step(step):
                items = items_of(step)
                last = len(items) - 1
                due = {k: [] for k in range(last + 1)}
                if step.place > 0:
                    tile, q = step.value - 1, (step.q - 1) % TPG
                    due[1].append(lambda: x2_out(tile, (step.place - 1) % 2))
                    at = S_AT_LAST if step.place == TILES - 1 else S_AT[step.q]
                    after_top = step.group if step.q == 1 and step.place > 1 else None
                    due[at[0] + LAG].append(lambda: x2_rows_out(tile, after_top))
                    for i in range(NBLK):
                        read = step.group if step.q == 1 and step.place > 1 else None
                        due[min(at[1 + i] + LAG, last)].append(lambda i=i, read=read: s_out(tile, q, i, read))
                if step.q == 0 and step.place > 0:
                    g = step.group - 1
                    due[L2_AT[-1] + LAG].append(lambda: r2_out(g))
                    due[min(TOP_AT[0] + LAG, last)].append(lambda: h1_out(g))
                    due[min(TOP_AT[1] + LAG, last)].append(lambda: h2_out(g))
                    due[min(TOP_AT[2] + LAG, last)].append(lambda: y_out_of(g))
                if step.q == 2 and step.place <= LAST_GATHER:
                    for dq in range(4):
                        due[PREP_AT[dq] + LAG].append(lambda dq=dq: columns_hi(step.group + 1, dq))
                if step.q == 3 and step.place < TILES - 1:
                    for i in range(2):
                        def rows_after_diag(i=i):
                            act.wait_ge(diag_in, step.value + 1)
                            rows(step.group + 1, i)
                        due[min(X0D_AT[i] + LAG, last)].append(rows_after_diag)
                if ("B", C0 - 1) in items:
                    k = items.index(("B", C0 - 1))
                    due[min(k + X1_LAG, last)].append(lambda k=k: x1_out(step, unit_of(step, k)))
                if step.q == 2:
                    act.wait_ge(rep_ready, reps_through(step.back(), 0))
                    act.wait_ge(cols_lo, step.group * 4 + 4)
                    act.wait_ge(cols_hi, step.group * 4 + 4)
                    copy(x0_last[:, :], x0_cols[:, 3 * COLS:4 * COLS]).then_inc(last_in, 1)
                for k, item in enumerate(items):
                    if item[0] == "A":
                        three(step, k)
                    if splits_at(item):
                        high_part(step, k)
                    for f in due[k]:
                        f()
                if step.q == 0 and step.place > 0:
                    act.wait_ge(h1_ready, step.group)
                act.wait_ge(r0_done, step.value + 1)
                copy(r0_sb[:, 32 * step.q:32 * step.q + 32], r0_tile[:, step.place % 2, :]).then_inc(r0_in, 1)

            act.wait_ge(weights_in, 80)
            copy(sel[:, :], sel_raw).then_inc(w_hi_done, 1)
            act.wait_ge(w0_sum, 1)
            copy(w0_hi[:, :, :], w0_raw).then_inc(w_hi_done, 1)
            act.wait_ge(w1_in, 16)
            copy(w1_hi[:, :, :], w1_raw).then_inc(w_hi_done, 1)
            act.wait_ge(blank, 1)
            for dq in range(4):
                columns_hi(0, dq)
            before = Step(-1, -1, -1)
            for k, item in enumerate(items_of(before)):
                if item == ("A", 0):
                    three(before, k)
                    for i in range(2):
                        rows(0, i)
                elif splits_at(item):
                    high_part(before, k)
            act.wait_ge(w_lo_done, 1)
            x1_out(before, UNITS - 1)
            act.wait_ge(x1_in, 1)
            turn_quadrants(act, 0, 1)
            run_steps(act, one_step)
            x2_out(TILES - 1, None)
            x2_rows_out(TILES - 1, None)
            for i in range(NBLK):
                s_out(TILES - 1, TPG - 1, i, None)
            r2_out(GROUPS - 1)
            h1_out(GROUPS - 1)
            h2_out(GROUPS - 1)
            y_out_of(GROUPS - 1)

        @block.vector
        def _(dve):
            def columns_lo(g, dq):
                dve.wait_ge(cols_hi, g * 4 + (dq + 1))
                d = slice(4 * dq, 4 * dq + 4)
                dve.tensor_tensor(block_view(x0_cols[LO:LO + F, :])[:, d],
                                  prep_bank(g, dq)[0:F, :].rearrange("p (d k b) -> p d k b", d=4, b=BLK),
                                  block_view(x0_cols[0:F, :].bitcast(F32))[:, d], ALU.subtract).then_inc(cols_lo, 1)

            def product(step, k):
                kind, n = items_of(step)[k]
                u = unit_of(step, k)
                b = bank(k)
                dve.wait_ge(rep_ready, reps_through(step, k))
                free_whole = step.place >= 0 and not (step.place == 0 and u == 0)
                if kind == "L1":
                    if n == 0:
                        dve.wait_ge(x1_turned, step.value * 96 + 96)
                    x1 = x1_rot[:, step.place % 2, :, :]
                    if free_whole:
                        dve.wait_ge(unit_done, units_through(step, u - 3))
                    dve.tensor_tensor(z_whole[:, ring(u), :], rep[b][:, :], x1[:, SPLIT, :], ALU.mult).then_inc(prod, 1)
                    wait_low(dve, step, u - 2)
                    dve.tensor_tensor(z[:, u % 2, :, :], rep[b][:, None, :].to_broadcast([P, SPLIT, COLS]),
                                      x1[:, 0:SPLIT, :], ALU.mult).then_inc(prod, 1)
                else:
                    if n == 0:
                        dve.wait_ge(three_in, step.value + 2)
                    if n == WHOLE0:
                        if free_whole:
                            dve.wait_ge(unit_done, units_through(step, u - 3))
                        dst = z_whole[:, ring(u), :]
                    else:
                        i = n if n < WHOLE0 else n - WHOLE0 - 1
                        if i == 0 and step.place >= 0:
                            wait_low(dve, step, u - 2)
                        dst = z[:, u % 2, i, :]
                    dve.tensor_tensor(dst, rep[b][:, :], x0_three[:, :], ALU.mult).then_inc(prod, 1)

            def low_part(step, u):
                dve.wait_ge(hi_third, units_through(step, u))
                if step.place >= 0 and not (step.place == 0 and u == 0):
                    dve.wait_ge(unit_done, units_through(step, u - 3))
                dve.tensor_tensor(z_lo[:, ring(u), 2, :], z[:, u % 2, 2, :], z_hi[:, ring(u), 2, :].bitcast(F32),
                                  ALU.subtract).then_inc(lo_dve, 1)

            def spread_rows(step):
                dve.wait_ge(rows_in, step.group * 2 + 2)
                if step.place > 0:
                    dve.wait_ge(s_ready, step.value * NBLK)
                q = step.q
                dve.tensor_tensor(diag[:, :, :, :],
                                  x0_rows[:, 4 * q:4 * q + 4, None, :].to_broadcast([P, NBLK, BLK, FS]),
                                  mask_sb[:, None, :, None].to_broadcast([P, NBLK, BLK, FS]),
                                  ALU.mult).then_inc(diag_in, 1)

            def sum_x1(step):
                dve.wait_ge(x1_in, step.value + 2)
                if step.place >= 1:
                    dve.wait_ge(r0_in, step.value)
                b = (step.place + 1) % 2
                dve.tensor_reduce(r0_tile[:, b, :].rearrange("p (k b) -> p k b", b=BLK),
                                  x1_rot[:, b, 0, :].rearrange("p (k d b) -> p k b d", d=D, b=BLK),
                                  AX_X, ALU.add).then_inc(r0_done, 1)

            def one_step(step):
                items = items_of(step)
                last = len(items) - 1
                due = {k: [] for k in range(last + 1)}
                due[min(DIAG_AT[step.q], last)].append(lambda: spread_rows(step))
                if step.q == 2 and step.place <= LAST_GATHER:
                    for dq in range(4):
                        due[min(PREP_AT[dq] + LAG + 1, last)].append(lambda dq=dq: columns_lo(step.group + 1, dq))
                if ("B", C0 - 1) in items:
                    due[min(items.index(("B", C0 - 1)) + 5, last)].append(lambda: sum_x1(step))
                for k, item in enumerate(items):
                    if item[0] != "A":
                        product(step, k)
                    if k > 0 and splits_at(items[k - 1]):
                        low_part(step, unit_of(step, k - 1))
                    elif k == 0 and step.place > 0:
                        low_part(step, -1)
                    for f in due[k]:
                        f()

            dve.memset(x0_cols[32:LO, :].bitcast(F32), 1.0).then_inc(blank, 1)
            dve.wait_ge(weights_in, 80)
            dve.tensor_tensor(w0_raw, w0a_raw, w0b_raw, ALU.add).then_inc(w0_sum, 1)
            dve.tensor_tensor(w0_whole[:, :], w0a_raw[:, WHOLE0, :], w0b_raw[:, WHOLE0, :], ALU.add).then_inc(w0_sum, 1)
            dve.wait_ge(w_hi_done, 2)
            dve.tensor_tensor(w0_lo[:, :, :], w0_raw, w0_hi[:, :, :].bitcast(F32), ALU.subtract).then_inc(w_lo_done, 1)
            dve.wait_ge(w_hi_done, 3)
            dve.tensor_tensor(w1_lo[:, :, :], w1_raw, w1_hi[:, :, :].bitcast(F32),
                              ALU.subtract).then_inc(w_lo_done, 1)
            for dq in range(4):
                columns_lo(0, dq)
            before = Step(-1, -1, -1)
            for k, item in enumerate(items_of(before)):
                if item is not None and item[0] == "B":
                    product(before, k)
            for u in range(FG, UNITS):
                low_part(before, u)
            sum_x1(before)
            run_steps(dve, one_step)
            low_part(Step(TILES - 1, TILES - 1, None), FG - 1)

        @block.tensor
        def _(pe):
            def columns_t(g, dq):
                for i in range(4):
                    mm = pe.matmul(prep_bank(g, dq)[0:F, i * P:(i + 1) * P], emb[:, :, 4 * dq + i], ident[:, :],
                                   start=True, stop=True)
                mm.then_inc(prep_t, 1)

            def rows_of(g, i):
                pe.wait_ge(cols_hi, g * 4 + 4)
                pe.wait_ge(cols_lo, g * 4 + 4)
                for k in range(8):
                    at = (8 * i + k) * P
                    mm = pe.matmul(side[i][:, k * FS:(k + 1) * FS], x0_cols[:, at:at + P], sel[:, NSEL * P:SEL_COLS],
                                   start=True, stop=True)
                mm.then_inc(rows_t, 1)

            def replicate(step, k):
                n_items = len(items_of(step))
                if k >= n_items:
                    if step.place == TILES - 1:
                        return
                    step = Step(step.value + 1, step.place + 1, None)
                    k -= n_items
                kind, n = items_of(step)[k]
                prev, j = (step, k - 3) if k >= 3 else (step.back(), k - 3 + ITEMS)
                old = items_of(prev)[j]
                if old is not None:
                    if old[0] == "A":
                        pe.wait_ge(three_in, prev.value + 2)
                    else:
                        pe.wait_ge(prod, products_through(prev, j))
                q = step.q if kind == "L1" else (step.q + 1) % TPG
                if kind == "A" and q == 0:
                    pe.wait_ge(cols_hi, step.group * 4 + 8)
                    pe.wait_ge(cols_lo, step.group * 4 + 8)
                cols = x0_last[:, :] if kind == "L1" and q == 3 else x0_cols[:, q * COLS:(q + 1) * COLS]
                which = {"L1": SEL_REP + n, "A": SEL_A, "B": SEL_B + n}[kind]
                pe.matmul(rep[bank(k)][:, :], sel[:, which * P:(which + 1) * P], cols,
                          start=True, stop=True).then_inc(rep_ready, 1)

            def contract(step, k, between=lambda: None):
                kind, n = items_of(step)[k]
                u = unit_of(step, k)
                s = ring(u)
                whole = True
                if kind == "L1":
                    acc, hi, lo, chunks = acc1[step.place % 2], w1_hi, w1_lo, range(SPLIT * n, SPLIT * n + SPLIT)
                    opens, closes, w_whole = n == 0, n == FG - 1, w1_whole[:, n, :]
                    if opens and step.place >= 2:
                        pe.wait_ge(x2_in, step.value - 1)
                else:
                    acc, hi, lo, chunks = acc0, w0_hi, w0_lo, (0, 1, 2) if n == WHOLE0 else (4, 5, 6)
                    opens, closes, w_whole = n == WHOLE0, n != WHOLE0, w0_whole[:, :]
                    whole = n == WHOLE0
                    if opens and step.place >= 0:
                        pe.wait_ge(x1_in, step.value + 1)
                if whole:
                    pe.wait_ge(prod, products_through(step, k, 0))
                    pe.matmul(acc[:, :], w_whole, z_whole[:, s, :], start=opens, stop=False)
                pe.wait_ge(hi_two, units_through(step, u))
                for i, c in enumerate(chunks):
                    if i == 2:
                        pe.wait_ge(hi_third, units_through(step, u))
                    pe.matmul(acc[:, :], hi[:, c, :], z_hi[:, s, i, :], start=False, stop=False)
                    pe.matmul(acc[:, :], lo[:, c, :], z_hi[:, s, i, :], start=False, stop=False)
                between()
                wait_low(pe, step, u)
                for i, c in enumerate(chunks):
                    mm = pe.matmul(acc[:, :], hi[:, c, :], z_lo[:, s, i, :], start=False,
                                   stop=closes and i == SPLIT - 1)
                mm.then_inc(unit_done, 1)

            def x2_transpose(value):
                pe.wait_ge(x2_in, value + 1)
                for i in range(NBLK):
                    mm = pe.transpose(side[0][:, i * P:(i + 1) * P], x2_sb[:, i * P:(i + 1) * P], ident[:, :])
                mm.then_inc(x2_t, 1)

            def s_block(value, i):
                if i == 0:
                    pe.wait_ge(x2_rows_in, value + 1)
                    pe.wait_ge(diag_in, value + 1)
                elif i > 1:
                    pe.wait_ge(s_in, value * NBLK + (i - 1))
                pe.matmul(side[(i + 1) % 2][:, 0:BLK * FS], x2_rows[:, i, :], diag[:, i, :, :].rearrange("p b f -> p (b f)"),
                          start=True, stop=True).then_inc(s_ready, 1)

            def layer2(g, i):
                if i == 0:
                    pe.wait_ge(s_in, g * (TPG * NBLK) + TPG * NBLK)
                    pe.wait_ge(top_in, 128)
                for f in range(L2_CUT[i], L2_CUT[i + 1]):
                    mm = pe.matmul(side[0][:, 0:P], w2_sb[:, f, :], s_sb[:, f, :], start=f == 0, stop=f == F - 1)
                if i == 2:
                    mm.then_inc(r2_ready, 1)

            def top1(g):
                pe.wait_ge(r2_in, g + 1)
                pe.wait_ge(r0_in, g * TPG + TPG)
                pe.wait_ge(dense_in, g * 16 + 16)
                for c in range(H1 // P):
                    cut = slice(c * P, (c + 1) * P)
                    for i, x in enumerate((r0_sb[:, :], s_sb[:, F, :], r2_sb[:, :])):
                        pe.matmul(side[1][:, cut], wt1_sb[:, i, cut], x, start=i == 0, stop=False)
                    mm = pe.matmul(side[1][:, cut], wt1_sb[0:16, 3, cut], dense_sb[:, :], start=False, stop=True)
                mm.then_inc(h1_ready, 1)

            def top2(g):
                pe.wait_ge(h1_in, g * 4 + 4)
                for c in range(H2 // P):
                    cut = slice(c * P, (c + 1) * P)
                    for i in range(H1 // P):
                        mm = pe.matmul(side[0][:, cut], wt2_sb[:, i, cut], h1_sb[:, i, :], start=i == 0, stop=i == 3)
                mm.then_inc(h2_ready, 1)

            def top3(g):
                pe.wait_ge(h2_in, g * 2 + 2)
                for i in range(H2 // P):
                    mm = pe.matmul(side[1][0:1, 0:P], wt3_sb[:, i:i + 1], h2_sb[:, i, :], start=i == 0, stop=i == 1)
                mm.then_inc(y_ready, 1)

            def one_step(step):
                items = items_of(step)
                jobs = {k: [] for k in range(len(items))}
                if step.q == 2:
                    jobs[len(items) - AHEAD - 1].append(lambda: pe.wait_ge(last_in, step.group + 1))
                if step.q == 2 and step.place <= LAST_GATHER:
                    g = step.group + 1

                    def prepare(dq):
                        if dq == 0:
                            pe.wait_ge(gathered, g * (16 * F) + 16 * F)
                        if dq < 2:
                            pe.wait_ge(s_in, step.value * NBLK)
                        else:
                            pe.wait_ge(cols_lo, g * 4 + (dq - 1))
                        columns_t(g, dq)

                    for dq in range(4):
                        jobs[PREP_AT[dq]].append(lambda dq=dq: prepare(dq))
                if step.q == 3 and step.place < TILES - 1:
                    g = step.group + 1

                    def tile_rows(i):
                        pe.wait_ge(s_in, step.value * NBLK)
                        rows_of(g, i)

                    for i in range(2):
                        jobs[X0D_AT[i]].append(lambda i=i: tile_rows(i))
                if step.place > 0:
                    tile = step.value - 1
                    at = S_AT_LAST if step.place == TILES - 1 else S_AT[step.q]

                    def turn():
                        if step.q == 3 and step.place < TILES - 1:
                            pe.wait_ge(cols_lo, step.group * 4 + 7)
                        elif step.q == 1 and step.place > 1:
                            pe.wait_ge(h2_in, step.group * 2)
                        elif step.q == 0:
                            pe.wait_ge(rows_in, step.group * 2 + 2)
                        elif step.place > 1:
                            pe.wait_ge(s_in, tile * NBLK)
                        x2_transpose(tile)

                    def first_block():
                        if step.q == 3 and step.place < TILES - 1:
                            pe.wait_ge(cols_lo, step.group * 4 + 8)
                        elif step.q == 1 and step.place > 1:
                            pe.wait_ge(y_in, step.group)
                        s_block(tile, 0)

                    jobs[at[0]].append(turn)
                    jobs[at[1]].append(first_block)
                    for i in range(1, NBLK):
                        jobs[at[1 + i]].append(lambda i=i: s_block(tile, i))
                if step.q == 0 and step.place > 0:
                    g0 = step.group - 1
                    for i in range(3):
                        jobs[L2_AT[i]].append(lambda i=i: layer2(g0, i))
                    for k, f in zip(TOP_AT, (top1, top2, top3)):
                        jobs[k].append(lambda f=f: f(g0))
                for k, item in enumerate(items):
                    if contracts_at(item):
                        contract(step, k, lambda: replicate(step, k + AHEAD))
                    else:
                        replicate(step, k + AHEAD)
                    for job in jobs[k]:
                        job()

            def keep_warm(n):
                for _ in range(n):
                    pe.matmul(acc0[:, :], sel[:, 0:P], sel[:, P:P + COLS], start=True, stop=True)

            pe.wait_ge(weights_in, 80)
            pe.wait_ge(w_hi_done, 2)
            pe.wait_ge(nearly, 1)
            keep_warm(WARM[0])
            pe.wait_ge(gathered, 16 * F)
            for dq in range(4):
                columns_t(0, dq)
            keep_warm(WARM[1])
            pe.wait_ge(cols_lo, 4)
            before = Step(-1, -1, -1)
            for k in range(FG, FG + 3):
                replicate(before, k)
            rows_of(0, 0)
            rows_of(0, 1)
            replicate(before, FG + 3)
            pe.wait_ge(w_lo_done, 2)
            pe.wait_ge(w0_sum, 2)
            pe.wait_ge(top_in, 128)
            for k in range(FG, ITEMS):
                if k + AHEAD < ITEMS + 3:
                    replicate(before, k + AHEAD)
                if contracts_at(items_of(before)[k]):
                    contract(before, k)
            pe.wait_ge(x1_in, 1)
            keep_warm(WARM[2])
            replicate(before, ITEMS + 3)
            run_steps(pe, one_step)
            pe.wait_ge(s_in, (TILES - 1) * NBLK)
            x2_transpose(TILES - 1)
            for i in range(NBLK):
                s_block(TILES - 1, i)
            for i in range(3):
                layer2(GROUPS - 1, i)
            top1(GROUPS - 1)
            top2(GROUPS - 1)
            top3(GROUPS - 1)


def selector_matrices():
    s = np.zeros((F + 1, SEL_COLS), np.float32)
    for g in range(FG):
        for j in range(4):
            if 4 * g + j < F:
                s[4 * g + j, (SEL_REP + g) * P + 32 * j:(SEL_REP + g) * P + 32 * j + 32] = 1.0
    for r in range(3):
        for f in range(F):
            s[f, SEL_A * P + F * r + f] = 1.0
    for c in range(C0):
        for r in range(3):
            if 3 * c + r <= F // 2:
                for f in range(F):
                    s[(f + 3 * c + r) % F, (SEL_B + c) * P + F * r + f] = 1.0
    for f in range(FS):
        s[f, NSEL * P + f] = 1.0
    full = np.zeros((P, SEL_COLS), np.float32)
    full[0:F + 1] = s
    full[LO:LO + F] = s[0:F]
    return full


def kernel(**inputs):
    import concourse.bacc as bacc
    from concourse.bass_utils import run_bass_kernel_spmd

    f0 = np.asarray(inputs["L0_rec_f0"]).reshape(F, F, M)
    f1 = np.asarray(inputs["L0_rec_f1"]).reshape(F, M, M)
    f2 = np.asarray(inputs["L0_rec_f2"]).reshape(F, M, M)
    w0a = np.zeros((P, C0, M), np.float32)
    w0b = np.zeros((P, C0, M), np.float32)
    for c in range(C0):
        for r in range(3):
            shift = 3 * c + r
            if shift <= F // 2:
                f = np.arange(F)
                w0a[F * r:F * r + F, c] = f0[f, (f + shift) % F]
                if shift:
                    w0b[F * r:F * r + F, c] = f0[(f + shift) % F, f]
    w1 = np.zeros((P, FG * SPLIT, M), np.float32)
    w1_w = np.zeros((P, FG, M), np.float32)
    for g in range(FG):
        for j in range(4):
            if 4 * g + j < F:
                for r in range(ROT):
                    at = 32 * ((j + r) % 4)
                    dst = w1[:, SPLIT * g + r] if r < SPLIT else w1_w[:, g]
                    dst[32 * j:32 * j + 32] = f1[4 * g + j, at:at + 32]
    position = np.arange(P)
    mask8 = (position[:, None] % BLK == np.arange(BLK)[None, :]).astype(np.float32)

    arrays = {
        "ids": np.asarray(inputs["ids"]),
        **{f"tbl_{f}": np.asarray(inputs[f"tbl_{f}"]) for f in range(F)},
        "w0a": w0a, "w0b": w0b, "w1": w1, "w1_w": w1_w,
        "w2": np.ascontiguousarray(f2.transpose(1, 0, 2)),
        "W_top1": np.asarray(inputs["W_top1"]),
        "b_top1": np.ascontiguousarray(np.asarray(inputs["b_top1"]).reshape(H1 // P, P).T),
        "W_top2": np.asarray(inputs["W_top2"]),
        "b_top2": np.ascontiguousarray(np.asarray(inputs["b_top2"]).reshape(H2 // P, P).T),
        "W_top3": np.ascontiguousarray(np.asarray(inputs["W_top3"]).reshape(H2 // P, P).T),
        "dense_t": np.ascontiguousarray(np.asarray(inputs["dense_ctx"]).T),
        "selectors": selector_matrices(),
        "identity": np.eye(P, dtype=np.float32),
        "mask8": mask8,
    }
    nc = bacc.Bacc("TRN2", target_bir_lowering=False, num_devices=1)
    ap = {name: nc.dram_tensor(f"in_{name}_dram", a.shape, mybir.dt.from_np(a.dtype), kind="ExternalInput").ap()
          for name, a in arrays.items()}
    y = nc.dram_tensor("out_0_dram", (B, 1), F32, kind="ExternalOutput").ap()
    cross_network(nc, ap["ids"], [ap[f"tbl_{f}"] for f in range(F)], ap["w0a"], ap["w0b"], ap["w1"], ap["w1_w"], ap["w2"],
                  ap["W_top1"], ap["b_top1"], ap["W_top2"], ap["b_top2"], ap["W_top3"], ap["dense_t"],
                  ap["selectors"], ap["identity"], ap["mask8"], y)
    r = run_bass_kernel_spmd(nc, [{f"in_{name}_dram": a for name, a in arrays.items()}], core_ids=[0])
    return r.results[0]["out_0_dram"]
```

```python
from contextlib import ExitStack

import numpy as np

import concourse.bass as bass
from concourse import mybir

F32 = mybir.dt.float32
F32R = mybir.dt.float32r
I32 = mybir.dt.int32
ALU = mybir.AluOpType
ACT = mybir.ActivationFunctionType
AX_X = mybir.AxisListType.X

B = 512
F = 39
D = 16
M = 128
P = 128
FEATURES = 3 * M + 16
H1, H2 = 512, 256

COLS = 512
SMALL = 10
ROWS = 125
CHUNKS = 10
BLK = 8
GROUPS = B // P
TPG = 4
TILES = GROUPS * TPG
NBLK = COLS // P
LO = 64
KX = LO + F
FG = 10
ROT = 4
C0 = 7
FS = F + 1

SEL_REP = 0
SEL_A = FG
SEL_B = FG + 1
NSEL = FG + 1 + C0
SEL_COLS = NSEL * P + FS

UNITS = FG + 2
SPLIT = 3
WHOLE0 = 3
ITEMS = FG + 1 + C0
AHEAD = 4


def items_of(step):
    cross = [("L1", g) for g in range(FG)]
    if step.place == TILES - 1:
        return cross
    if step.place < 0:
        return [None] * FG + [("A", 0)] + [("B", c) for c in range(C0)]
    first = L0_AT[step.q]
    second = first + L0_APART
    return (cross[:first] + [("A", 0)] + [("B", c) for c in range(WHOLE0 + 1)] + cross[first:second] +
            [("B", c) for c in range(WHOLE0 + 1, C0)] + cross[second:])


def unit_of(step, k):
    return sum(contracts_at(item) for item in items_of(step)[:k]) + (FG if step.place < 0 else 0)


def splits_at(item):
    return item is not None and (item[0] == "L1" or item in (("B", 2), ("B", C0 - 1)))


def contracts_at(item):
    return item is not None and (item[0] == "L1" or item in (("B", WHOLE0), ("B", C0 - 1)))


class Step:

    def __init__(self, value, place, group):
        self.value, self.place, self.group = value, place, group

    @property
    def q(self):
        return self.place % TPG

    def back(self, n=1):
        return Step(self.value - n, self.place - n, None)


def units_through(step, u):
    return step.value * UNITS + (2 + u + 1)


def reps_through(step, k):
    return step.value * ITEMS + (1 + C0 + k + 1)


def products_through(step, k, part=1):
    count = {"L1": 2, "A": 0, "B": 1}
    names = items_of(step)[:k + 1]
    here = sum(count[it[0]] for it in names if it is not None)
    if names[-1] is not None and names[-1][0] == "L1" and part == 0:
        here -= 1
    if step.place < 0:
        return here
    return step.value * (2 * FG + C0) + (C0 + here)


def gathers_of(step):
    if step.place > LAST_GATHER:
        return (0,) * UNITS, F
    if step.place < TPG - 1:
        return GATHER_EARLY[step.place], F - sum(sum(x) for x in GATHER_EARLY[step.place:])
    order = (3, 0, 1, 2)
    return GATHER_AT[step.q], sum(sum(GATHER_AT[x]) for x in order[:order.index(step.q)])


def ring(u):
    return u % 3


def bank(k):
    return (1 + C0 + k) % 3


S_AT_LAST = (1, 2, 3, 4, 5)
L0_AT = (4, 4, 4, 4)
L0_APART = 0
S_AT = {0: (1, 3, 4, 5, 6), 1: (1, 3, 5, 7, 9), 2: (1, 3, 5, 7, 9), 3: (1, 3, 5, 7, 9)}
L2_AT = (8, 10, 11)
TOP_AT = (13, 15, 17)
PREP_AT = (13, 13, 15, 15)
X0D_AT = (13, 14)
L2_CUT = (0, 13, 26, F)
DIAG_AT = {0: (11, 13), 1: (13, 15), 2: (13, 15), 3: (12, 16)}
LAG = 2
X1_LAG = 1
WARM = (16, 7, 2, 1)
GATHER_AT = {
    3: (0, 0, 1, 1, 1, 1, 1, 1, 1, 1, 1, 0),
    0: (1, 1, 1, 1, 2, 2, 1, 2, 2, 2, 2, 1),
    1: (0, 1, 1, 0, 1, 1, 1, 1, 0, 1, 1, 0),
    2: (0, 1, 0, 1, 1, 1, 0, 0, 0, 0, 0, 0),
}
GATHER_FIRST = 10
GATHER_EARLY = (
    (0, 1, 1, 1, 1, 1, 0, 1, 0, 1, 1, 0),
    (0, 1, 0, 1, 1, 1, 1, 1, 0, 1, 1, 0),
    (0, 1, 1, 1, 1, 1, 0, 0, 0, 0, 0, 0),
)
LAST_GATHER = 2 * TPG - 2


def small_fields(tables):
    return sorted(range(len(tables)), key=lambda f: tables[f].shape[0])[:SMALL]


def cross_network(nc, ids, ids_small, row_numbers, small_tables, tables, w0a, w0b, w1, w1_w, w2, wt1, bt1, wt2, bt2, wt3, dense_t, selectors, identity, mask8, out):
    with ExitStack() as ctx:
        def sb(name, shape, dt=F32):
            return ctx.enter_context(nc.sbuf_tensor(name, shape, dt))

        def ps(name, shape):
            return ctx.enter_context(nc.psum_tensor(name, shape, F32))

        def sem(name):
            return ctx.enter_context(nc.semaphore(name))

        w1_hi = sb("w1_hi", [P, FG * SPLIT, M], F32R)
        w1_lo = sb("w1_lo", [P, FG * SPLIT, M], F32R)
        w1_whole = sb("w1_whole", [P, FG, M])
        w0_hi = sb("w0_hi", [P, C0, M], F32R)
        w0_lo = sb("w0_lo", [P, C0, M], F32R)
        w0_whole = sb("w0_whole", [P, M])
        w2_sb = sb("w2_sb", [P, F, M])
        wt1_sb = sb("wt1_sb", [P, 4, H1])
        wt2_sb = sb("wt2_sb", [P, H1 // P, H2])
        wt3_sb = sb("wt3_sb", [P, H2 // P])
        bt1_sb = sb("bt1_sb", [P, H1 // P])
        bt2_sb = sb("bt2_sb", [P, H2 // P])
        sel = sb("sel", [KX, SEL_COLS], F32R)
        ident_twice = sb("ident_twice", [P, 2 * P])
        ident = ident_twice[:, 0:P]
        mask_sb = sb("mask_sb", [P, BLK])
        numbers = sb("numbers", [ROWS, CHUNKS])
        tick = sb("tick", [1, 1])
        ids_now = sb("ids_now", [P, F], I32)
        ids_second = sb("ids_second", [P, F], I32)
        emb = sb("emb", [P, F, D])
        emb_second = sb("emb_second", [P, F, D])
        x0_cols = sb("x0_cols", [KX, TPG * COLS], F32R)
        x0_last = sb("x0_last", [KX, COLS], F32R)
        x0_three = sb("x0_three", [P, COLS])
        x0_rows = sb("x0_rows", [P, TPG * NBLK, FS])
        z = sb("z", [P, 2, SPLIT, COLS])
        z_whole = sb("z_whole", [P, 3, COLS])
        z_hi = sb("z_hi", [P, 3, SPLIT, COLS], F32R)
        z_lo = sb("z_lo", [P, 3, SPLIT, COLS], F32R)
        x1_rot = sb("x1_rot", [P, 2, ROT, COLS])
        x2_sb = sb("x2_sb", [P, COLS])
        x2_rows = sb("x2_rows", [P, NBLK, P])
        diag = sb("diag", [P, NBLK, BLK, FS])
        s_sb = sb("s_sb", [P, FS, P])
        r0_tile = sb("r0_tile", [P, 2, NBLK * BLK])
        r0_sb = sb("r0_sb", [P, P])
        r2_sb = sb("r2_sb", [P, P])
        dense_sb = sb("dense_sb", [16, P])
        h1_sb = x2_rows
        h2_sb = sb("h2_sb", [P, H2 // P, P])
        y_sb = sb("y_sb", [1, P])

        w1_raw = s_sb[:, 0:FG * SPLIT, :]
        zf = z[:, :, :, :].rearrange("p a b n -> p (a b n)")
        w0a_raw = x1_rot[:, 0, :, :].rearrange("p a n -> p (a n)")[:, 0:C0 * M].rearrange("p (c m) -> p c m", c=C0)
        w0b_raw = x1_rot[:, 0, :, :].rearrange("p a n -> p (a n)")[:, C0 * M:2 * C0 * M].rearrange("p (c m) -> p c m", c=C0)
        w0_raw = x1_rot[:, 1, :, :].rearrange("p a n -> p (a n)")[:, 0:C0 * M].rearrange("p (c m) -> p c m", c=C0)
        sel_raw = zf[0:KX, 0:SEL_COLS]

        w2_flat = w2_sb[:, :, :].rearrange("p f m -> p (f m)")
        small_ids = w2_flat[0:ROWS, 0:SMALL * P].rearrange("p (s b) -> p s b", b=P)
        small_rows = w2_flat[0:ROWS, SMALL * P:SMALL * P + SMALL * CHUNKS * D].rearrange(
            "p (s c d) -> p s c d", c=CHUNKS, d=D)
        ids_spread = wt1_sb[:, :, :].rearrange("p a b -> p (a b)")[0:ROWS, 0:SMALL * P].bitcast(I32).rearrange(
            "p (s b) -> p s b", b=P)
        small_parts = z_hi[:, :, :, :].rearrange("p a b n -> p (a b n)")[0:ROWS, 0:SMALL * CHUNKS * 2 * D].rearrange(
            "p (s c d) -> p s c d", c=CHUNKS, d=2 * D)
        chosen = z_lo[:, :, :, :].rearrange("p a b n -> p (a b n)")[0:ROWS, 0:3 * CHUNKS * P].rearrange(
            "p (a c b) -> p a c b", c=CHUNKS, b=P)

        rep = [ps(f"rep{i}", [P, COLS]) for i in range(3)]
        acc0 = ps("acc0", [P, COLS])
        acc1 = [ps(f"acc1_{i}", [P, COLS]) for i in range(2)]
        side = [ps("side_t", [P, COLS]), ps("side_s", [P, COLS])]

        ids_in = sem("ids_in")
        second_in = sem("second_in")
        weights_in = sem("weights_in")
        w1_in = sem("w1_in")
        whole_in = sem("whole_in")
        nearly = sem("nearly")
        top_in = sem("top_in")
        dense_in = sem("dense_in")
        blank = sem("blank")
        small_in = sem("small_in")
        ids_real = sem("ids_real")
        is_row = sem("is_row")
        looked_up = sem("looked_up")
        small_done = sem("small_done")
        small_hi = sem("small_hi")
        small_lo = sem("small_lo")
        tables_in = sem("tables_in")
        w0_sum = sem("w0_sum")
        w_hi_done = sem("w_hi_done")
        w_lo_done = sem("w_lo_done")
        gathered = sem("gathered")
        gathered_second = sem("gathered_second")
        prep_t = sem("prep_t")
        cols_hi = sem("cols_hi")
        cols_lo = sem("cols_lo")
        rows_t = sem("rows_t")
        rows_in = sem("rows_in")
        last_in = sem("last_in")
        rep_ready = sem("rep_ready")
        three_in = sem("three_in")
        prod = sem("prod")
        hi_two = sem("hi_two")
        hi_third = sem("hi_third")
        lo_pool = sem("lo_pool")
        lo_dve = sem("lo_dve")
        unit_done = sem("unit_done")
        x1_in = sem("x1_in")
        x1_turned = sem("x1_turned")
        first_t = sem("first_t")
        first_in = sem("first_in")
        r0_done = sem("r0_done")
        r0_in = sem("r0_in")
        x2_in = sem("x2_in")
        x2_t = sem("x2_t")
        x2_rows_in = sem("x2_rows_in")
        diag_in = sem("diag_in")
        s_ready = sem("s_ready")
        s_in = sem("s_in")
        r2_ready = sem("r2_ready")
        r2_in = sem("r2_in")
        h1_ready = sem("h1_ready")
        h1_in = sem("h1_in")
        h2_ready = sem("h2_ready")
        h2_in = sem("h2_in")
        y_ready = sem("y_ready")
        y_in = sem("y_in")
        y_out = sem("y_out")

        small = small_fields(tables)

        def prep_bank(g, dq):
            first = isinstance(g, int) and g == 0
            return (side + acc1)[dq] if first else side[dq % 2]

        h1_last = rep + [acc0]
        first_turn = {3: acc1[1], 1: side[0], 2: side[1]}

        block = ctx.enter_context(nc.Block())

        def run_steps(eng, step_of):
            for n in range(TPG - 1):
                step_of(Step(n, n, 0))
            with eng.Fori(0, GROUPS - 2) as g:
                for n in range(TPG - 1, 2 * TPG - 1):
                    step_of(Step(g * TPG + n, n, g + n // TPG))
            for n in range(TILES - TPG - 1, TILES):
                step_of(Step(n, n, n // TPG))

        def wait_low(eng, step, u):
            eng.wait_ge(lo_pool, units_through(step, u))
            eng.wait_ge(lo_dve, units_through(step, u))

        @block.sync
        def _(sp):
            def turn_x1(value, b):
                sp.wait_ge(x1_in, value + 1)
                for r in range(1, ROT):
                    cut = P - 32 * r
                    sp.dma_start(x1_rot[0:cut, b, r, :], x1_rot[32 * r:P, b, 0, :]).then_inc(x1_turned, 16)
                    sp.dma_start(x1_rot[cut:P, b, r, :], x1_rot[0:32 * r, b, 0, :]).then_inc(x1_turned, 16)

            def store_y(g):
                sp.wait_ge(y_in, g + 1)
                sp.dma_start(out[bass.ds(g * P, P), :].rearrange("b o -> o b"), y_sb[:, :]).then_inc(y_out, 16)

            def load_dense(g):
                sp.dma_start(dense_sb[:, :], dense_t[:, bass.ds(g * P, P)]).then_inc(dense_in, 16)

            def load_ids(g):
                sp.dma_start(ids_now[:, :], ids[bass.ds(g * P, P), :]).then_inc(ids_in, 16)

            load_ids(0)
            sp.dma_start(ids_second[:, :], ids[P:2 * P, :]).then_inc(second_in, 16)
            sp.dma_start(ids_spread, ids_small.partition_broadcast(ROWS)).then_inc(small_in, 16)
            sp.dma_start(numbers[:, :], row_numbers).then_inc(small_in, 16)
            sp.dma_start(small_rows, small_tables).then_inc(tables_in, 16)
            sp.dma_start(sel_raw, selectors[0:KX, :]).then_inc(weights_in, 16)
            sp.dma_start(w0a_raw, w0a).then_inc(weights_in, 16)
            sp.dma_start(w0b_raw, w0b).then_inc(weights_in, 16)
            sp.dma_start(ident_twice[:, :], identity).then_inc(weights_in, 16)
            sp.dma_start(mask_sb[:, :], mask8).then_inc(weights_in, 16)
            sp.dma_start(w1_raw, w1).then_inc(w1_in, 16)
            sp.dma_start(w1_whole[:, :, :], w1_w).then_inc(whole_in, 16)
            sp.wait_ge(ids_real, 1)
            sp.dma_start(wt1_sb[:, 0:3, :], wt1[0:3 * P, :].rearrange("(c p) n -> p c n", p=P)).then_inc(top_in, 16)
            sp.dma_start(wt1_sb[0:16, 3, :], wt1[3 * P:FEATURES, :]).then_inc(top_in, 16)
            sp.dma_start(wt2_sb[:, :, :], wt2.rearrange("(c p) n -> p c n", p=P)).then_inc(top_in, 16)
            sp.dma_start(wt3_sb[:, :], wt3).then_inc(top_in, 16)
            sp.dma_start(bt1_sb[:, :], bt1).then_inc(top_in, 16)
            sp.dma_start(bt2_sb[:, :], bt2).then_inc(top_in, 16)
            load_dense(0)
            sp.wait_ge(is_row, SMALL)
            sp.dma_start(w2_sb[:, :, :], w2).then_inc(top_in, 16)

            def one_step(step):
                if step.q == 3 and step.place <= LAST_GATHER:
                    sp.wait_ge(gathered, step.group * (16 * F) + 16 * (F - SMALL))
                    load_ids(step.group + 2)
                if step.place < TILES - 1:
                    turn_x1(step.value + 1, (step.place + 1) % 2)
                if step.q == 0 and step.place > 0:
                    store_y(step.group - 1)
                    sp.wait_ge(y_out, step.group * 16)
                    load_dense(step.group)

            run_steps(sp, one_step)
            store_y(GROUPS - 1)
            sp.wait_ge(y_out, 16 * GROUPS)

        @block.gpsimd
        def _(pool):
            def gather(f, ids_of=ids_now, rows=emb):
                pool.indirect_dma_start(
                    out=rows[:, f, :], out_offset=None, in_=tables[f][:, :],
                    in_offset=bass.IndirectOffsetOnAxis(ap=ids_of[:, f:f + 1], axis=0),
                ).then_inc(gathered if rows is emb else gathered_second, 16)

            def low_part(step, u):
                pool.wait_ge(hi_two, units_through(step, u))
                if step.place >= 0 and not (step.place == 0 and u == 0):
                    pool.wait_ge(unit_done, units_through(step, u - 3))
                pool.tensor_tensor(z_lo[:, ring(u), 0:2, :], z[:, u % 2, 0:2, :], z_hi[:, ring(u), 0:2, :].bitcast(F32),
                                   ALU.subtract).then_inc(lo_pool, 1)

            def one_step(step):
                counts, fields = gathers_of(step)
                for u in range(FG if step.place == TILES - 1 else UNITS):
                    if counts[u] and step.q == 3 and not any(counts[:u]):
                        pool.wait_ge(prep_t, step.group * 4 + 8)
                        pool.wait_ge(ids_in, step.group * 16 + 32)
                    low_part(step, u)
                    for f in range(fields + sum(counts[:u]), fields + sum(counts[:u + 1])):
                        if step.place < TPG - 1:
                            gather(f, ids_second, emb_second)
                        else:
                            gather(f)

            pool.wait_ge(ids_in, 16)
            others = [f for f in range(F) if f not in small]
            for f in others:
                if f == others[-5]:
                    pool.memset(tick[:, :], 0.0).then_inc(nearly, 1)
                gather(f)
            pool.wait_ge(second_in, 16)
            for f in range(GATHER_FIRST):
                gather(f, ids_second, emb_second)
            before = Step(-1, -1, -1)
            for u in range(FG, UNITS):
                low_part(before, u)
            for f in range(GATHER_FIRST, gathers_of(Step(0, 0, 0))[1]):
                gather(f, ids_second, emb_second)
            run_steps(pool, one_step)

        def block_view(ap):
            return ap.rearrange("p (k d b) -> p d k b", d=D, b=BLK)

        @block.scalar
        def _(act):
            def copy(dst, src):
                return act.activation(dst, src, ACT.Copy)

            def columns_hi(g, dq):
                act.wait_ge(prep_t, g * 4 + (dq + 1))
                copy(block_view(x0_cols[0:F, :])[:, 4 * dq:4 * dq + 4],
                     prep_bank(g, dq)[0:F, :].rearrange("p (d k b) -> p d k b", d=4, b=BLK)).then_inc(cols_hi, 1)

            def rows(g, i):
                act.wait_ge(rows_t, g * 2 + (i + 1))
                copy(x0_rows[:, 8 * i:8 * i + 8, :],
                     side[i][:, 0:8 * FS].rearrange("p (k f) -> p k f", f=FS)).then_inc(rows_in, 1)

            def three(step, k):
                act.wait_ge(rep_ready, reps_through(step, k))
                if step.place >= 0:
                    prev = step.back()
                    act.wait_ge(prod, products_through(prev, items_of(prev).index(("B", C0 - 1))))
                copy(x0_three[:, :], rep[bank(k)][:, :]).then_inc(three_in, 1)

            def high_part(step, k):
                u = unit_of(step, k)
                one_by_one = items_of(step)[k][0] == "B"
                act.wait_ge(prod, products_through(step, k - 1 if one_by_one else k))
                if step.place >= 0 and not (step.place == 0 and u == 0):
                    act.wait_ge(unit_done, units_through(step, u - 3))
                copy(z_hi[:, ring(u), 0:2, :], z[:, u % 2, 0:2, :]).then_inc(hi_two, 1)
                if one_by_one:
                    act.wait_ge(prod, products_through(step, k))
                copy(z_hi[:, ring(u), 2, :], z[:, u % 2, 2, :]).then_inc(hi_third, 1)

            def x1_out(step, u):
                act.wait_ge(unit_done, units_through(step, u))
                if step.place >= 1:
                    act.wait_ge(prod, products_through(step.back(), ITEMS - 1))
                copy(x1_rot[:, (step.place + 1) % 2, 0, :], acc0[:, :]).then_inc(x1_in, 1)

            def x2_out(value, b):
                act.wait_ge(unit_done, value * UNITS + (2 + UNITS) if b is not None else 2 + UNITS * value + FG)
                if not (isinstance(value, int) and value == 0):
                    act.wait_ge(x2_t, value)
                copy(x2_sb[:, :], acc1[b if b is not None else value % 2][:, :]).then_inc(x2_in, 1)

            def x2_rows_out(value, after_top):
                act.wait_ge(x2_t, value + 1)
                if not (isinstance(value, int) and value == 0):
                    act.wait_ge(s_ready, value * NBLK)
                if after_top is not None:
                    act.wait_ge(h2_ready, after_top)
                copy(x2_rows[:, :, :], side[0][:, :].rearrange("p (k m) -> p k m", m=P)).then_inc(x2_rows_in, 1)

            def s_out(value, q, blk, groups_read):
                act.wait_ge(s_ready, value * NBLK + (blk + 1))
                if groups_read is not None:
                    act.wait_ge(r2_ready, groups_read)
                    act.wait_ge(h1_ready, groups_read)
                at = 32 * q + BLK * blk
                copy(s_sb[:, :, at:at + BLK],
                     side[(blk + 1) % 2][:, 0:BLK * FS].rearrange("p (b f) -> p f b", f=FS)).then_inc(s_in, 1)

            def r2_out(g):
                act.wait_ge(r2_ready, g + 1)
                copy(r2_sb[:, :], side[0][:, 0:P]).then_inc(r2_in, 1)

            def h1_out(g):
                last = isinstance(g, int) and g == GROUPS - 1
                for c in range(H1 // P):
                    act.wait_ge(h1_ready, g + 1 + (c if last else 0))
                    act.activation(h1_sb[:, c, :], h1_last[c][:, 0:P] if last else side[1][:, c * P:(c + 1) * P], ACT.Relu,
                                   bias=bt1_sb[:, c:c + 1]).then_inc(h1_in, 1)

            def h2_out(g):
                act.wait_ge(h2_ready, g + 1)
                for c in range(H2 // P):
                    act.activation(h2_sb[:, c, :], side[0][:, c * P:(c + 1) * P], ACT.Relu,
                                   bias=bt2_sb[:, c:c + 1]).then_inc(h2_in, 1)

            def y_out_of(g):
                act.wait_ge(y_ready, g + 1)
                copy(y_sb[:, :], side[1][0:1, 0:P]).then_inc(y_in, 1)

            def one_step(step):
                items = items_of(step)
                last = len(items) - 1
                due = {k: [] for k in range(last + 1)}
                if step.place > 0:
                    tile, q = step.value - 1, (step.q - 1) % TPG
                    due[1].append(lambda: x2_out(tile, (step.place - 1) % 2))
                    at = S_AT_LAST if step.place == TILES - 1 else S_AT[step.q]
                    after_top = step.group if step.q == 1 and step.place > 1 else None
                    due[at[0] + LAG].append(lambda: x2_rows_out(tile, after_top))
                    for i in range(NBLK):
                        read = step.group if step.q == 1 and step.place > 1 else None
                        due[min(at[1 + i] + LAG, last)].append(lambda i=i, read=read: s_out(tile, q, i, read))
                if step.q == 0 and step.place > 0:
                    g = step.group - 1
                    due[L2_AT[-1] + LAG].append(lambda: r2_out(g))
                    due[min(TOP_AT[0] + LAG, last)].append(lambda: h1_out(g))
                    due[min(TOP_AT[1] + LAG, last)].append(lambda: h2_out(g))
                if step.q == 1 and step.place > 1:
                    due[0].append(lambda: y_out_of(step.group - 1))
                if step.q == 2 and step.place <= LAST_GATHER:
                    for dq in range(4):
                        due[PREP_AT[dq] + LAG].append(lambda dq=dq: columns_hi(step.group + 1, dq))
                if step.q == 3 and step.place < TILES - 1:
                    for i in range(2):
                        def rows_after_diag(i=i):
                            act.wait_ge(diag_in, step.value * 2 + 2)
                            rows(step.group + 1, i)
                        due[min(X0D_AT[i] + LAG, last)].append(rows_after_diag)
                if ("B", C0 - 1) in items:
                    k = items.index(("B", C0 - 1))
                    due[min(k + X1_LAG, last)].append(lambda k=k: x1_out(step, unit_of(step, k)))
                if step.q == 2:
                    act.wait_ge(rep_ready, reps_through(step.back(), 0))
                    act.wait_ge(cols_lo, step.group * 4 + 4)
                    act.wait_ge(cols_hi, step.group * 4 + 4)
                    copy(x0_last[:, :], x0_cols[:, 3 * COLS:4 * COLS]).then_inc(last_in, 1)
                for k, item in enumerate(items):
                    if item[0] == "A":
                        three(step, k)
                    if splits_at(item):
                        high_part(step, k)
                    for f in due[k]:
                        f()
                if step.q == 0 and step.place > 0:
                    act.wait_ge(h1_ready, step.group)
                act.wait_ge(r0_done, step.value + 1)
                copy(r0_sb[:, 32 * step.q:32 * step.q + 32], r0_tile[:, step.place % 2, :]).then_inc(r0_in, 1)

            act.wait_ge(small_in, 32)
            copy(small_ids, ids_spread).then_inc(ids_real, 1)
            act.wait_ge(tables_in, 16)
            copy(small_parts[:, :, :, 0:D], small_rows).then_inc(small_hi, 1)
            act.wait_ge(weights_in, 80)
            copy(sel[:, :], sel_raw).then_inc(w_hi_done, 1)
            act.wait_ge(w0_sum, 1)
            copy(w0_hi[:, :, :], w0_raw).then_inc(w_hi_done, 1)
            act.wait_ge(w1_in, 16)
            copy(w1_hi[:, :, :], w1_raw).then_inc(w_hi_done, 1)
            act.wait_ge(blank, 1)
            for dq in range(4):
                columns_hi(0, dq)
            before = Step(-1, -1, -1)
            for k, item in enumerate(items_of(before)):
                if item == ("A", 0):
                    three(before, k)
                elif splits_at(item):
                    high_part(before, k)
            act.wait_ge(w_lo_done, 1)
            x1_out(before, UNITS - 1)
            for i, (r, turned) in enumerate(first_turn.items()):
                act.wait_ge(first_t, i + 1)
                copy(x1_rot[:, 0, r, :], turned[:, :]).then_inc(first_in, 1)
            for i in range(2):
                rows(0, i)
            run_steps(act, one_step)
            x2_out(TILES - 1, None)
            x2_rows_out(TILES - 1, None)
            for i in range(NBLK):
                s_out(TILES - 1, TPG - 1, i, None)
            r2_out(GROUPS - 1)
            h1_out(GROUPS - 1)
            h2_out(GROUPS - 1)
            y_out_of(GROUPS - 1)

        @block.vector
        def _(dve):
            def columns_lo(g, dq):
                dve.wait_ge(cols_hi, g * 4 + (dq + 1))
                d = slice(4 * dq, 4 * dq + 4)
                dve.tensor_tensor(block_view(x0_cols[LO:LO + F, :])[:, d],
                                  prep_bank(g, dq)[0:F, :].rearrange("p (d k b) -> p d k b", d=4, b=BLK),
                                  block_view(x0_cols[0:F, :].bitcast(F32))[:, d], ALU.subtract).then_inc(cols_lo, 1)

            def product(step, k):
                kind, n = items_of(step)[k]
                u = unit_of(step, k)
                b = bank(k)
                dve.wait_ge(rep_ready, reps_through(step, k))
                free_whole = step.place >= 0 and not (step.place == 0 and u == 0)
                if kind == "L1":
                    if n == 0 and step.place == 0:
                        dve.wait_ge(first_in, 1)
                    elif n == 0:
                        dve.wait_ge(x1_turned, step.value * 96)
                    x1 = x1_rot[:, step.place % 2, :, :]
                    if free_whole:
                        dve.wait_ge(unit_done, units_through(step, u - 3))
                    dve.tensor_tensor(z_whole[:, ring(u), :], rep[b][:, :], x1[:, SPLIT, :], ALU.mult).then_inc(prod, 1)
                    wait_low(dve, step, u - 2)
                    if n == 0 and step.place == 0:
                        dve.wait_ge(first_in, 3)
                    dve.tensor_tensor(z[:, u % 2, :, :], rep[b][:, None, :].to_broadcast([P, SPLIT, COLS]),
                                      x1[:, 0:SPLIT, :], ALU.mult).then_inc(prod, 1)
                else:
                    if n == 0:
                        dve.wait_ge(three_in, step.value + 2)
                    if n == WHOLE0:
                        if free_whole:
                            dve.wait_ge(unit_done, units_through(step, u - 3))
                        dst = z_whole[:, ring(u), :]
                    else:
                        i = n if n < WHOLE0 else n - WHOLE0 - 1
                        if i == 0 and step.place >= 0:
                            wait_low(dve, step, u - 2)
                        dst = z[:, u % 2, i, :]
                    dve.tensor_tensor(dst, rep[b][:, :], x0_three[:, :], ALU.mult).then_inc(prod, 1)

            def low_part(step, u):
                dve.wait_ge(hi_third, units_through(step, u))
                if step.place >= 0 and not (step.place == 0 and u == 0):
                    dve.wait_ge(unit_done, units_through(step, u - 3))
                dve.tensor_tensor(z_lo[:, ring(u), 2, :], z[:, u % 2, 2, :], z_hi[:, ring(u), 2, :].bitcast(F32),
                                  ALU.subtract).then_inc(lo_dve, 1)

            def spread_rows(step, half):
                dve.wait_ge(rows_in, step.group * 2 + 2)
                if step.place > 0:
                    dve.wait_ge(s_ready, step.value * NBLK)
                n, at = NBLK // 2, NBLK // 2 * half
                row = NBLK * step.q + at
                dve.tensor_tensor(diag[:, at:at + n, :, :],
                                  x0_rows[:, row:row + n, None, :].to_broadcast([P, n, BLK, FS]),
                                  mask_sb[:, None, :, None].to_broadcast([P, n, BLK, FS]),
                                  ALU.mult).then_inc(diag_in, 1)

            def sum_x1(step):
                dve.wait_ge(x1_in, step.value + 2)
                if step.place >= 1:
                    dve.wait_ge(r0_in, step.value)
                b = (step.place + 1) % 2
                dve.tensor_reduce(r0_tile[:, b, :].rearrange("p (k b) -> p k b", b=BLK),
                                  x1_rot[:, b, 0, :].rearrange("p (k d b) -> p k b d", d=D, b=BLK),
                                  AX_X, ALU.add).then_inc(r0_done, 1)

            def one_step(step):
                items = items_of(step)
                last = len(items) - 1
                due = {k: [] for k in range(last + 1)}
                for half in range(2):
                    due[min(DIAG_AT[step.q][half], last)].append(lambda half=half: spread_rows(step, half))
                if step.q == 2 and step.place <= LAST_GATHER:
                    for dq in range(4):
                        due[min(PREP_AT[dq] + LAG + 1, last)].append(lambda dq=dq: columns_lo(step.group + 1, dq))
                if ("B", C0 - 1) in items:
                    due[min(items.index(("B", C0 - 1)) + 5, last)].append(lambda: sum_x1(step))
                for k, item in enumerate(items):
                    if item[0] != "A":
                        product(step, k)
                    if k > 0 and splits_at(items[k - 1]):
                        low_part(step, unit_of(step, k - 1))
                    elif k == 0 and step.place > 0:
                        low_part(step, -1)
                    for f in due[k]:
                        f()

            dve.memset(x0_cols[32:LO, :].bitcast(F32), 1.0).then_inc(blank, 1)

            def choose(i):
                n = tables[small[i]].shape[0] // ROWS
                if i > 2:
                    dve.wait_ge(looked_up, i - 2)
                dve.tensor_tensor(chosen[:, i % 3, 0:n, :], small_ids[:, i, None, :].to_broadcast([ROWS, n, P]),
                                  numbers[:, 0:n, None].to_broadcast([ROWS, n, P]), ALU.is_equal).then_inc(is_row, 1)

            def add_parts(i):
                dve.wait_ge(looked_up, i + 1)
                dve.tensor_reduce(emb[:, small[i], :], rep[i % 3][:, 0:2 * D].rearrange("p (h d) -> p d h", h=2),
                                  AX_X, ALU.add).then_inc(small_done, 1)

            dve.wait_ge(ids_real, 1)
            choose(0)
            choose(1)
            dve.wait_ge(small_hi, 1)
            dve.tensor_tensor(small_parts[:, :, :, D:2 * D], small_rows, small_parts[:, :, :, 0:D].bitcast(F32),
                              ALU.subtract).then_inc(small_lo, 1)
            choose(2)
            dve.wait_ge(weights_in, 80)
            dve.tensor_tensor(w0_raw, w0a_raw, w0b_raw, ALU.add).then_inc(w0_sum, 1)
            dve.tensor_tensor(w0_whole[:, :], w0a_raw[:, WHOLE0, :], w0b_raw[:, WHOLE0, :], ALU.add).then_inc(w0_sum, 1)
            for i in range(3, SMALL):
                choose(i)
                add_parts(i - 3)
            for i in range(SMALL - 3, SMALL):
                add_parts(i)
            dve.wait_ge(w_hi_done, 2)
            dve.tensor_tensor(w0_lo[:, :, :], w0_raw, w0_hi[:, :, :].bitcast(F32), ALU.subtract).then_inc(w_lo_done, 1)
            for dq in range(4):
                columns_lo(0, dq)
            before = Step(-1, -1, -1)
            for k, item in enumerate(items_of(before)):
                if item is not None and item[0] == "B":
                    product(before, k)
            for u in range(FG, UNITS):
                low_part(before, u)
            dve.wait_ge(w_hi_done, 3)
            dve.tensor_tensor(w1_lo[:, :, :], w1_raw, w1_hi[:, :, :].bitcast(F32),
                              ALU.subtract).then_inc(w_lo_done, 1)
            sum_x1(before)
            run_steps(dve, one_step)
            low_part(Step(TILES - 1, TILES - 1, None), FG - 1)

        @block.tensor
        def _(pe):
            def columns_t(g, dq):
                rows = emb_second if isinstance(g, int) and g == 1 else emb
                for i in range(4):
                    mm = pe.matmul(prep_bank(g, dq)[0:F, i * P:(i + 1) * P], rows[:, :, 4 * dq + i], ident[:, :],
                                   start=True, stop=True)
                mm.then_inc(prep_t, 1)

            def rows_of(g, i):
                pe.wait_ge(cols_hi, g * 4 + 4)
                pe.wait_ge(cols_lo, g * 4 + 4)
                for k in range(8):
                    at = (8 * i + k) * P
                    mm = pe.matmul(side[i][:, k * FS:(k + 1) * FS], x0_cols[:, at:at + P], sel[:, NSEL * P:SEL_COLS],
                                   start=True, stop=True)
                mm.then_inc(rows_t, 1)

            def replicate(step, k):
                n_items = len(items_of(step))
                if k >= n_items:
                    if step.place == TILES - 1:
                        return
                    step = Step(step.value + 1, step.place + 1, None)
                    k -= n_items
                kind, n = items_of(step)[k]
                prev, j = (step, k - 3) if k >= 3 else (step.back(), k - 3 + ITEMS)
                old = items_of(prev)[j]
                if old is not None:
                    if old[0] == "A":
                        pe.wait_ge(three_in, prev.value + 2)
                    else:
                        pe.wait_ge(prod, products_through(prev, j))
                q = step.q if kind == "L1" else (step.q + 1) % TPG
                if kind == "A" and q == 0:
                    pe.wait_ge(cols_hi, step.group * 4 + 8)
                    pe.wait_ge(cols_lo, step.group * 4 + 8)
                cols = x0_last[:, :] if kind == "L1" and q == 3 else x0_cols[:, q * COLS:(q + 1) * COLS]
                which = {"L1": SEL_REP + n, "A": SEL_A, "B": SEL_B + n}[kind]
                pe.matmul(rep[bank(k)][:, :], sel[:, which * P:(which + 1) * P], cols,
                          start=True, stop=True).then_inc(rep_ready, 1)

            def contract(step, k, between=lambda: None):
                kind, n = items_of(step)[k]
                u = unit_of(step, k)
                s = ring(u)
                whole = True
                if kind == "L1":
                    acc, hi, lo, chunks = acc1[step.place % 2], w1_hi, w1_lo, range(SPLIT * n, SPLIT * n + SPLIT)
                    opens, closes, w_whole = n == 0, n == FG - 1, w1_whole[:, n, :]
                    if opens and step.place >= 2:
                        pe.wait_ge(x2_in, step.value - 1)
                else:
                    acc, hi, lo, chunks = acc0, w0_hi, w0_lo, (0, 1, 2) if n == WHOLE0 else (4, 5, 6)
                    opens, closes, w_whole = n == WHOLE0, n != WHOLE0, w0_whole[:, :]
                    whole = n == WHOLE0
                    if opens and step.place >= 0:
                        pe.wait_ge(x1_in, step.value + 1)
                if whole:
                    pe.wait_ge(prod, products_through(step, k, 0))
                    pe.matmul(acc[:, :], w_whole, z_whole[:, s, :], start=opens, stop=False)
                pe.wait_ge(hi_two, units_through(step, u))
                for i, c in enumerate(chunks):
                    if i == 2:
                        pe.wait_ge(hi_third, units_through(step, u))
                    pe.matmul(acc[:, :], hi[:, c, :], z_hi[:, s, i, :], start=False, stop=False)
                    pe.matmul(acc[:, :], lo[:, c, :], z_hi[:, s, i, :], start=False, stop=False)
                between()
                wait_low(pe, step, u)
                for i, c in enumerate(chunks):
                    mm = pe.matmul(acc[:, :], hi[:, c, :], z_lo[:, s, i, :], start=False,
                                   stop=closes and i == SPLIT - 1)
                mm.then_inc(unit_done, 1)

            def x2_transpose(value):
                pe.wait_ge(x2_in, value + 1)
                for i in range(NBLK):
                    mm = pe.transpose(side[0][:, i * P:(i + 1) * P], x2_sb[:, i * P:(i + 1) * P], ident[:, :])
                mm.then_inc(x2_t, 1)

            def s_block(value, i):
                if i == 0:
                    pe.wait_ge(x2_rows_in, value + 1)
                    pe.wait_ge(diag_in, value * 2 + 2)
                elif i > 1:
                    pe.wait_ge(s_in, value * NBLK + (i - 1))
                pe.matmul(side[(i + 1) % 2][:, 0:BLK * FS], x2_rows[:, i, :], diag[:, i, :, :].rearrange("p b f -> p (b f)"),
                          start=True, stop=True).then_inc(s_ready, 1)

            def layer2(g, i):
                if i == 0:
                    pe.wait_ge(s_in, g * (TPG * NBLK) + TPG * NBLK)
                    pe.wait_ge(top_in, 112)
                for f in range(L2_CUT[i], L2_CUT[i + 1]):
                    mm = pe.matmul(side[0][:, 0:P], w2_sb[:, f, :], s_sb[:, f, :], start=f == 0, stop=f == F - 1)
                if i == 2:
                    mm.then_inc(r2_ready, 1)

            def top1(g):
                pe.wait_ge(r2_in, g + 1)
                pe.wait_ge(r0_in, g * TPG + TPG)
                pe.wait_ge(dense_in, g * 16 + 16)
                for c in range(H1 // P):
                    cut = slice(c * P, (c + 1) * P)
                    for i, x in enumerate((r0_sb[:, :], s_sb[:, F, :], r2_sb[:, :])):
                        pe.matmul(side[1][:, cut], wt1_sb[:, i, cut], x, start=i == 0, stop=False)
                    mm = pe.matmul(side[1][:, cut], wt1_sb[0:16, 3, cut], dense_sb[:, :], start=False, stop=True)
                mm.then_inc(h1_ready, 1)

            def top1_begins(columns):
                pe.wait_ge(r0_in, TILES)
                pe.wait_ge(dense_in, GROUPS * 16)
                for c in columns:
                    cut = slice(c * P, (c + 1) * P)
                    pe.matmul(h1_last[c][:, 0:P], wt1_sb[:, 0, cut], r0_sb[:, :], start=True, stop=False)
                    pe.matmul(h1_last[c][:, 0:P], wt1_sb[0:16, 3, cut], dense_sb[:, :], start=False, stop=False)

            def top1_ends():
                pe.wait_ge(r2_in, GROUPS)
                for c in range(H1 // P):
                    cut = slice(c * P, (c + 1) * P)
                    pe.matmul(h1_last[c][:, 0:P], wt1_sb[:, 1, cut], s_sb[:, F, :], start=False, stop=False)
                    pe.matmul(h1_last[c][:, 0:P], wt1_sb[:, 2, cut], r2_sb[:, :], start=False,
                              stop=True).then_inc(h1_ready, 1)

            def top2(g):
                pe.wait_ge(h1_in, g * 4 + 4)
                for c in range(H2 // P):
                    cut = slice(c * P, (c + 1) * P)
                    for i in range(H1 // P):
                        mm = pe.matmul(side[0][:, cut], wt2_sb[:, i, cut], h1_sb[:, i, :], start=i == 0, stop=i == 3)
                mm.then_inc(h2_ready, 1)

            def top3(g):
                pe.wait_ge(h2_in, g * 2 + 2)
                for i in range(H2 // P):
                    mm = pe.matmul(side[1][0:1, 0:P], wt3_sb[:, i:i + 1], h2_sb[:, i, :], start=i == 0, stop=i == 1)
                mm.then_inc(y_ready, 1)

            def one_step(step):
                items = items_of(step)
                jobs = {k: [] for k in range(len(items))}
                if step.q == 2:
                    jobs[len(items) - AHEAD - 1].append(lambda: pe.wait_ge(last_in, step.group + 1))
                if step.q == 2 and step.place <= LAST_GATHER:
                    g = step.group + 1

                    def prepare(dq):
                        if dq == 0 and step.place < TPG:
                            pe.wait_ge(gathered_second, 16 * F)
                        elif dq == 0:
                            pe.wait_ge(gathered, g * (16 * F) - 16 * SMALL)
                        if dq < 2:
                            pe.wait_ge(s_in, step.value * NBLK)
                        else:
                            pe.wait_ge(cols_lo, g * 4 + (dq - 1))
                        columns_t(g, dq)

                    for dq in range(4):
                        jobs[PREP_AT[dq]].append(lambda dq=dq: prepare(dq))
                if step.q == 3 and step.place < TILES - 1:
                    g = step.group + 1

                    def tile_rows(i):
                        pe.wait_ge(s_in, step.value * NBLK)
                        rows_of(g, i)

                    for i in range(2):
                        jobs[X0D_AT[i]].append(lambda i=i: tile_rows(i))
                if step.place > 0:
                    tile = step.value - 1
                    at = S_AT_LAST if step.place == TILES - 1 else S_AT[step.q]

                    def turn():
                        if step.q == 3 and step.place < TILES - 1:
                            pe.wait_ge(cols_lo, step.group * 4 + 7)
                        elif step.q == 1 and step.place > 1:
                            pe.wait_ge(h2_in, step.group * 2)
                        elif step.q == 0:
                            pe.wait_ge(rows_in, step.group * 2 + 2)
                        elif step.place > 1:
                            pe.wait_ge(s_in, tile * NBLK)
                        else:
                            pe.wait_ge(rows_in, 2)
                        x2_transpose(tile)

                    def first_block():
                        if step.q == 3 and step.place < TILES - 1:
                            pe.wait_ge(cols_lo, step.group * 4 + 8)
                        elif step.q == 1 and step.place > 1:
                            pe.wait_ge(y_in, step.group)
                        s_block(tile, 0)

                    jobs[at[0]].append(turn)
                    jobs[at[1]].append(first_block)
                    for i in range(1, NBLK):
                        jobs[at[1 + i]].append(lambda i=i: s_block(tile, i))
                if step.q == 0 and step.place > 0:
                    g0 = step.group - 1
                    for i in range(3):
                        jobs[L2_AT[i]].append(lambda i=i: layer2(g0, i))
                    for k, f in zip(TOP_AT, (top1, top2, top3)):
                        jobs[k].append(lambda f=f: f(g0))
                for k, item in enumerate(items):
                    if contracts_at(item):
                        contract(step, k, lambda: replicate(step, k + AHEAD))
                    else:
                        replicate(step, k + AHEAD)
                    for job in jobs[k]:
                        job()

            def keep_warm(n):
                for _ in range(n):
                    pe.matmul(acc0[:, :], sel[:, 0:P], sel[:, P:P + COLS], start=True, stop=True)

            pe.wait_ge(small_lo, 1)
            for i, f in enumerate(small):
                n = tables[f].shape[0] // ROWS
                pe.wait_ge(is_row, i + 1)
                if i > 2:
                    pe.wait_ge(small_done, i - 2)
                for c in range(n):
                    mm = pe.matmul(rep[i % 3][:, 0:2 * D], chosen[:, i % 3, c, :], small_parts[:, i, c, :],
                                   start=c == 0, stop=c == n - 1)
                mm.then_inc(looked_up, 1)
            pe.wait_ge(weights_in, 80)
            pe.wait_ge(w_hi_done, 2)
            pe.wait_ge(nearly, 1)
            keep_warm(WARM[0])
            pe.wait_ge(gathered, 16 * (F - SMALL))
            pe.wait_ge(small_done, SMALL)
            for dq in range(4):
                columns_t(0, dq)
            keep_warm(WARM[1])
            pe.wait_ge(cols_lo, 4)
            before = Step(-1, -1, -1)
            for k in range(FG, FG + 3):
                replicate(before, k)
            replicate(before, FG + 3)
            pe.wait_ge(w_lo_done, 1)
            pe.wait_ge(w0_sum, 2)
            for k in range(FG, ITEMS):
                if k + AHEAD < ITEMS + 3:
                    replicate(before, k + AHEAD)
                if k < FG + 4:
                    keep_warm(WARM[3])
                if contracts_at(items_of(before)[k]):
                    contract(before, k)
            pe.wait_ge(x1_in, 1)
            for r, turned in first_turn.items():
                pe.matmul(turned[:, :], ident_twice[:, 32 * r:32 * r + P], x1_rot[:, 0, 0, :],
                          start=True, stop=True).then_inc(first_t, 1)
            keep_warm(WARM[2])
            pe.wait_ge(first_in, 3)
            rows_of(0, 0)
            rows_of(0, 1)
            replicate(before, ITEMS + 3)
            pe.wait_ge(w_lo_done, 2)
            pe.wait_ge(whole_in, 16)
            run_steps(pe, one_step)
            pe.wait_ge(s_in, (TILES - 1) * NBLK)
            top1_begins((0, 1))
            x2_transpose(TILES - 1)
            top1_begins((2, 3))
            for i in range(NBLK):
                s_block(TILES - 1, i)
            for i in range(3):
                layer2(GROUPS - 1, i)
            top1_ends()
            top2(GROUPS - 1)
            top3(GROUPS - 1)


def selector_matrices():
    s = np.zeros((F + 1, SEL_COLS), np.float32)
    for g in range(FG):
        for j in range(4):
            if 4 * g + j < F:
                s[4 * g + j, (SEL_REP + g) * P + 32 * j:(SEL_REP + g) * P + 32 * j + 32] = 1.0
    for r in range(3):
        for f in range(F):
            s[f, SEL_A * P + F * r + f] = 1.0
    for c in range(C0):
        for r in range(3):
            if 3 * c + r <= F // 2:
                for f in range(F):
                    s[(f + 3 * c + r) % F, (SEL_B + c) * P + F * r + f] = 1.0
    for f in range(FS):
        s[f, NSEL * P + f] = 1.0
    full = np.zeros((P, SEL_COLS), np.float32)
    full[0:F + 1] = s
    full[LO:LO + F] = s[0:F]
    return full


def kernel(**inputs):
    import concourse.bacc as bacc
    from concourse.bass_utils import run_bass_kernel_spmd

    f0 = np.asarray(inputs["L0_rec_f0"]).reshape(F, F, M)
    f1 = np.asarray(inputs["L0_rec_f1"]).reshape(F, M, M)
    f2 = np.asarray(inputs["L0_rec_f2"]).reshape(F, M, M)
    w0a = np.zeros((P, C0, M), np.float32)
    w0b = np.zeros((P, C0, M), np.float32)
    for c in range(C0):
        for r in range(3):
            shift = 3 * c + r
            if shift <= F // 2:
                f = np.arange(F)
                w0a[F * r:F * r + F, c] = f0[f, (f + shift) % F]
                if shift:
                    w0b[F * r:F * r + F, c] = f0[(f + shift) % F, f]
    w1 = np.zeros((P, FG * SPLIT, M), np.float32)
    w1_w = np.zeros((P, FG, M), np.float32)
    for g in range(FG):
        for j in range(4):
            if 4 * g + j < F:
                for r in range(ROT):
                    at = 32 * ((j + r) % 4)
                    dst = w1[:, SPLIT * g + r] if r < SPLIT else w1_w[:, g]
                    dst[32 * j:32 * j + 32] = f1[4 * g + j, at:at + 32]
    position = np.arange(P)
    tables = [np.asarray(inputs[f"tbl_{f}"]) for f in range(F)]
    small = small_fields(tables)
    small_tables = np.zeros((ROWS, SMALL, CHUNKS, D), np.float32)
    for i, f in enumerate(small):
        small_tables[:, i, 0:tables[f].shape[0] // ROWS] = tables[f].reshape(-1, ROWS, D).transpose(1, 0, 2)
    ids_small = np.ascontiguousarray(np.asarray(inputs["ids"]).T[small, 0:P])
    row_numbers = (np.arange(CHUNKS)[None, :] * ROWS + np.arange(ROWS)[:, None]).astype(np.float32)
    mask8 = (position[:, None] % BLK == np.arange(BLK)[None, :]).astype(np.float32)

    arrays = {
        "ids": np.asarray(inputs["ids"]),
        "ids_small": ids_small, "row_numbers": row_numbers, "small_tables": small_tables,
        **{f"tbl_{f}": np.asarray(inputs[f"tbl_{f}"]) for f in range(F)},
        "w0a": w0a, "w0b": w0b, "w1": w1, "w1_w": w1_w,
        "w2": np.ascontiguousarray(f2.transpose(1, 0, 2)),
        "W_top1": np.asarray(inputs["W_top1"]),
        "b_top1": np.ascontiguousarray(np.asarray(inputs["b_top1"]).reshape(H1 // P, P).T),
        "W_top2": np.asarray(inputs["W_top2"]),
        "b_top2": np.ascontiguousarray(np.asarray(inputs["b_top2"]).reshape(H2 // P, P).T),
        "W_top3": np.ascontiguousarray(np.asarray(inputs["W_top3"]).reshape(H2 // P, P).T),
        "dense_t": np.ascontiguousarray(np.asarray(inputs["dense_ctx"]).T),
        "selectors": selector_matrices(),
        "identity": np.tile(np.eye(P, dtype=np.float32), (1, 2)),
        "mask8": mask8,
    }
    nc = bacc.Bacc("TRN2", target_bir_lowering=False, num_devices=1)
    ap = {name: nc.dram_tensor(f"in_{name}_dram", a.shape, mybir.dt.from_np(a.dtype), kind="ExternalInput").ap()
          for name, a in arrays.items()}
    y = nc.dram_tensor("out_0_dram", (B, 1), F32, kind="ExternalOutput").ap()
    cross_network(nc, ap["ids"], ap["ids_small"], ap["row_numbers"], ap["small_tables"], [ap[f"tbl_{f}"] for f in range(F)], ap["w0a"], ap["w0b"], ap["w1"], ap["w1_w"], ap["w2"],
                  ap["W_top1"], ap["b_top1"], ap["W_top2"], ap["b_top2"], ap["W_top3"], ap["dense_t"],
                  ap["selectors"], ap["identity"], ap["mask8"], y)
    r = run_bass_kernel_spmd(nc, [{f"in_{name}_dram": a for name, a in arrays.items()}], core_ids=[0])
    return r.results[0]["out_0_dram"]
```
